# Optimizing a Trainium2 kernel written in Bass

```python
import numpy as np
import jax
import jax.numpy as jnp

def _softmax(x, axis=-1):
    return jax.nn.softmax(x, axis=axis)

def _gelu(x):
    return jax.nn.gelu(x, approximate=True)

def _silu(x):
    return jax.nn.silu(x)

def _sigmoid(x):
    return jax.nn.sigmoid(x)

def _layernorm(x, axis=-1, eps=1e-05):
    m = jnp.mean(x, axis=axis, keepdims=True)
    v = jnp.var(x, axis=axis, keepdims=True)
    return (x - m) / jnp.sqrt(v + eps)

def _scatter_add(tgt, idx, src, axis=0):
    return tgt.at[idx].add(src)

def _segment_sum(src, seg, n):
    return jax.ops.segment_sum(src, seg, n)
kernel_name = 'mk_seq_preln_d1_jaxref_r8_0cb931'

def setup_inputs(seed: int=0):
    np.random.seed(seed)
    _w = jnp.asarray

    def _L0_attn_setup():
        import jax, jax.numpy as jnp
        import numpy as np
        DIM = 128
        STATE = 128
        BATCH, SEQ = (4, 512)
        key = jax.random.key(seed)
        ks = jax.random.split(key, 12)
        s = 1.0 / np.sqrt(DIM)
        s4 = 1.0 / np.sqrt(DIM // 4)
        ss = 1.0 / np.sqrt(STATE)
        inp = {'x': jax.random.normal(ks[0], (BATCH, SEQ, DIM), dtype=jnp.float32), 'W_B': jax.random.uniform(ks[1], (DIM, STATE), minval=-s, maxval=s), 'b_B': jax.random.uniform(ks[2], (STATE,), minval=-s, maxval=s), 'W_C': jax.random.uniform(ks[3], (DIM, STATE), minval=-s, maxval=s), 'b_C': jax.random.uniform(ks[4], (STATE,), minval=-s, maxval=s), 'W_dt1': jax.random.uniform(ks[5], (DIM, DIM // 4), minval=-s, maxval=s), 'b_dt1': jax.random.uniform(ks[6], (DIM // 4,), minval=-s, maxval=s), 'W_dt2': jax.random.uniform(ks[7], (DIM // 4, STATE), minval=-s4, maxval=s4), 'b_dt2': jnp.full((STATE,), -4.0, dtype=jnp.float32), 'omega_base': jax.random.normal(ks[8], (STATE,)) * 0.1, 'D': jnp.ones((DIM,), dtype=jnp.float32), 'W_out': jax.random.uniform(ks[9], (STATE, DIM), minval=-ss, maxval=ss), 'b_out': jax.random.uniform(ks[10], (DIM,), minval=-ss, maxval=ss)}
        return inp
    _L0_attn_in = _L0_attn_setup()

    def _L0_ffn_setup():
        import jax, jax.numpy as jnp
        import numpy as np
        NUM_EXPERTS = 8
        TOP_K = 2
        FIXED_IDX = 0
        D_MODEL = 128
        D_FF = 512
        B, S = (4, 256)

        def _route(flat_x, Wr):
            logits = flat_x @ Wr.T
            probs = jax.nn.softmax(logits.astype(jnp.float32), axis=-1).astype(flat_x.dtype)
            fixed_probs = probs[:, FIXED_IDX:FIXED_IDX + 1]
            remaining = probs[:, 1:]
            other_probs, other_local = jax.lax.top_k(remaining, TOP_K - 1)
            other_idx = other_local + 1
            topk_idx = jnp.concatenate([jnp.full((flat_x.shape[0], 1), FIXED_IDX, dtype=jnp.int32), other_idx], axis=1)
            topk_probs = jnp.concatenate([fixed_probs, other_probs], axis=1)
            topk_probs = topk_probs / jnp.clip(topk_probs.sum(axis=-1, keepdims=True), 1e-09)
            gates = jnp.sum(jax.nn.one_hot(topk_idx, NUM_EXPERTS, dtype=topk_probs.dtype) * topk_probs[..., None], axis=1)
            return gates
        key = jax.random.key(seed)
        ks = jax.random.split(key, 5)
        scale_r = 1.0 / np.sqrt(D_MODEL)
        return {'x': jax.random.normal(ks[0], (B, S, D_MODEL), dtype=jnp.float32), 'Wr': jax.random.normal(ks[1], (NUM_EXPERTS, D_MODEL), dtype=jnp.float32) * scale_r, 'W1': jax.random.normal(ks[2], (NUM_EXPERTS, D_FF, D_MODEL), dtype=jnp.float32) * scale_r, 'W2': jax.random.normal(ks[3], (NUM_EXPERTS, D_MODEL, D_FF), dtype=jnp.float32) * (1.0 / np.sqrt(D_FF)), 'W3': jax.random.normal(ks[4], (NUM_EXPERTS, D_FF, D_MODEL), dtype=jnp.float32) * scale_r}
    _L0_ffn_in = _L0_ffn_setup()
    _d = {'L0_attn_x': _L0_attn_in['x'], 'L0_attn_W_B': _L0_attn_in['W_B'], 'L0_attn_b_B': _L0_attn_in['b_B'], 'L0_attn_W_C': _L0_attn_in['W_C'], 'L0_attn_b_C': _L0_attn_in['b_C'], 'L0_attn_W_dt1': _L0_attn_in['W_dt1'], 'L0_attn_b_dt1': _L0_attn_in['b_dt1'], 'L0_attn_W_dt2': _L0_attn_in['W_dt2'], 'L0_attn_b_dt2': _L0_attn_in['b_dt2'], 'L0_attn_omega_base': _L0_attn_in['omega_base'], 'L0_attn_D': _L0_attn_in['D'], 'L0_attn_W_out': _L0_attn_in['W_out'], 'L0_attn_b_out': _L0_attn_in['b_out'], 'L0_ffn_Wr': _L0_ffn_in['Wr'], 'L0_ffn_W1': _L0_ffn_in['W1'], 'L0_ffn_W2': _L0_ffn_in['W2'], 'L0_ffn_W3': _L0_ffn_in['W3']}
    _x0 = _d['L0_attn_x']
    _d['L0_attn_x'] = jax.random.normal(jax.random.fold_in(jax.random.key(seed), 1), (4, 512, 128), dtype=_x0.dtype)
    del _x0
    return _d

def reference(L0_attn_x, L0_attn_W_B, L0_attn_b_B, L0_attn_W_C, L0_attn_b_C, L0_attn_W_dt1, L0_attn_b_dt1, L0_attn_W_dt2, L0_attn_b_dt2, L0_attn_omega_base, L0_attn_D, L0_attn_W_out, L0_attn_b_out, L0_ffn_Wr, L0_ffn_W1, L0_ffn_W2, L0_ffn_W3):

    def _L0_attn_ref(x, W_B, b_B, W_C, b_C, W_dt1, b_dt1, W_dt2, b_dt2, omega_base, D, W_out, b_out):
        import jax, jax.numpy as jnp
        import numpy as np
        DIM = 128
        STATE = 128
        BATCH, SEQ = (4, 512)
        Bm = x @ W_B + b_B
        Cm = x @ W_C + b_C
        dt = jax.nn.softplus((x @ W_dt1 + b_dt1) @ W_dt2 + b_dt2)
        omega = omega_base * dt
        phi = jnp.cumsum(omega, axis=1)
        content = Bm * x[..., :STATE]
        cphi, sphi = (jnp.cos(phi), jnp.sin(phi))
        memory_real = jnp.cumsum(content * cphi, axis=1)
        memory_imag = jnp.cumsum(content * sphi, axis=1)
        retrieved = Cm * (memory_real * cphi + memory_imag * sphi)
        y = retrieved @ W_out + b_out + D * x
        return y

    def _L0_ffn_ref(x, Wr, W1, W2, W3):
        import jax, jax.numpy as jnp
        import numpy as np
        NUM_EXPERTS = 8
        TOP_K = 2
        FIXED_IDX = 0
        D_MODEL = 128
        D_FF = 512
        B, S = (4, 256)

        def _route(flat_x, Wr):
            logits = flat_x @ Wr.T
            probs = jax.nn.softmax(logits.astype(jnp.float32), axis=-1).astype(flat_x.dtype)
            fixed_probs = probs[:, FIXED_IDX:FIXED_IDX + 1]
            remaining = probs[:, 1:]
            other_probs, other_local = jax.lax.top_k(remaining, TOP_K - 1)
            other_idx = other_local + 1
            topk_idx = jnp.concatenate([jnp.full((flat_x.shape[0], 1), FIXED_IDX, dtype=jnp.int32), other_idx], axis=1)
            topk_probs = jnp.concatenate([fixed_probs, other_probs], axis=1)
            topk_probs = topk_probs / jnp.clip(topk_probs.sum(axis=-1, keepdims=True), 1e-09)
            gates = jnp.sum(jax.nn.one_hot(topk_idx, NUM_EXPERTS, dtype=topk_probs.dtype) * topk_probs[..., None], axis=1)
            return gates
        batch, seq, d_model = x.shape
        flat_x = x.reshape(batch * seq, d_model)
        gates = _route(flat_x, Wr)
        out = jnp.zeros_like(flat_x)
        for e in range(NUM_EXPERTS):
            h = jax.nn.silu(flat_x @ W1[e].T) * (flat_x @ W3[e].T)
            out = out + gates[:, e:e + 1] * (h @ W2[e].T)
        return out.reshape(batch, seq, d_model)
    x = L0_attn_x
    x = x + _L0_attn_ref(_layernorm(x, axis=-1), L0_attn_W_B, L0_attn_b_B, L0_attn_W_C, L0_attn_b_C, L0_attn_W_dt1, L0_attn_b_dt1, L0_attn_W_dt2, L0_attn_b_dt2, L0_attn_omega_base, L0_attn_D, L0_attn_W_out, L0_attn_b_out)
    x = x + _L0_ffn_ref(_layernorm(x, axis=-1), L0_ffn_Wr, L0_ffn_W1, L0_ffn_W2, L0_ffn_W3)
    return x

_drawn_inputs = setup_inputs


def setup_inputs(seed=0):
    import zlib

    import numpy as np

    out = dict(_drawn_inputs(seed))
    spreads = {'L0_attn_b_dt2': (-4.0, 0.2), 'L0_attn_D': (1.0, 0.2)}
    factors = {'L0_attn_W_dt1': 6.366,
     'L0_attn_b_dt1': 6.72,
     'L0_attn_W_dt2': 4.269,
     'L0_attn_b_out': 4.36}
    for name, (base, spread) in spreads.items():
        noise = np.random.default_rng([zlib.crc32(name.encode()), seed]).standard_normal(out[name].shape)
        drawn = base * np.exp(spread * noise) if base else spread * noise
        out[name] = jnp.asarray(drawn.astype(out[name].dtype))
    for name, factor in factors.items():
        out[name] = (out[name] * factor).astype(out[name].dtype)
    return out
```

```python
from contextlib import ExitStack
import math

import numpy as np

import concourse.bass as bass
from concourse import mybir

P = 128
F32 = mybir.dt.float32
BF16 = mybir.dt.bfloat16
I32 = mybir.dt.int32
U32 = mybir.dt.uint32
ALU = mybir.AluOpType
ACT = mybir.ActivationFunctionType
AX = mybir.AxisListType

BATCH, SEQ, DIM = 4, 512, 128
TOKENS = BATCH * SEQ
NT = TOKENS // P
TB = SEQ // P
EXPERTS, FF = 8, 512
NE = EXPERTS - 1
KF = FF // P
TILES = (TOKENS + NE * (P - 1)) // P
SLOTS = TILES * P
ROW = DIM + 2
TOKENS_OFF = 2 * TOKENS
EPS = 1e-5
MAGIC = 1.5 * 2.0 ** 23
TWO_PI = 6.283185


def build(nc, x, vecs, b_dt1, rows, w_b, w_c, w_dt1t, w_dt2, w_out, w_rt, w1t, w3t, w2t, out, scratch):
    with ExitStack() as ctx:
        def sb(name, shape, dt=F32):
            return ctx.enter_context(nc.sbuf_tensor(name, shape, dt))

        def sem(name):
            return ctx.enter_context(nc.semaphore(name))

        bank = [ctx.enter_context(nc.psum_tensor(f"bank{i}", [P, 512], F32)) for i in range(8)]

        wB, wC, wO = sb("wB", [P, DIM]), sb("wC", [P, DIM]), sb("wO", [P, DIM])
        wd1t, wd2, bd1 = sb("wd1t", [32, DIM]), sb("wd2", [32, DIM]), sb("bd1", [32, 1])
        wdt, bdt = sb("wdt", [P, DIM]), sb("bdt", [P, 1])
        wR = sb("wR", [P, EXPERTS])
        W1, W3, W2 = sb("W1", [P, EXPERTS * FF]), sb("W3", [P, EXPERTS * FF]), sb("W2", [P, EXPERTS * FF])
        vec = sb("vec", [P, 4])
        turn = sb("turn", [P, 1])
        half_pi = sb("half_pi", [P, 1])
        row = sb("row", [P, 2, DIM])
        ident = sb("ident", [P, P])
        tri = sb("tri", [P, P], BF16)
        ones_bf = sb("ones_bf", [P, P], BF16)
        minus_half = sb("minus_half", [P, NT])
        xt = sb("xt", [P, NT, DIM])
        st = sb("st", [P, NT, 6])
        mean, rstd, vpe = sb("mean", [P, NT]), sb("rstd", [P, NT]), sb("vpe", [P, NT])
        t_a, t_b, t_c = sb("t_a", [P, NT]), sb("t_b", [P, NT]), sb("t_c", [P, NT])
        xn = sb("xn", [P, TB, DIM])
        xnD = sb("xnD", [P, TB, DIM])
        spare = sb("spare", [P, 1])
        xnT = sb("xnT", [P, TOKENS])
        r_pos = sb("r_pos", [P, TOKENS])
        r_abs = sb("r_abs", [P, SEQ])
        r_log = sb("r_log", [P, TOKENS])
        cont = sb("cont", [P, TOKENS])
        CmT = sb("CmT", [P, TOKENS])
        names = ("cum", "kph", "tph", "nf", "naf", "sn", "cs", "cc", "csn", "mr", "mi", "ret")
        cum, kph, tph, nf, naf, sn, cs, cc, csn, mr, mi, ret = (sb(n, [P, SEQ]) for n in names)
        one = sb("one", [P, SEQ])
        x2 = sb("x2", [P, NT, DIM])
        xn2 = sb("xn2", [P, TB, DIM])
        xn2T = sb("xn2T", [P, SEQ])
        pay = sb("pay", [P, NT, ROW])
        lg = sb("lg", [P, NT, EXPERTS])
        sil = sb("sil", [P, 2, FF])
        hT0 = sb("hT0", [P, KF, SEQ])
        y0 = sb("y0", [P, NT, DIM])
        ex, eq, oh, pos3 = sb("ex", [P, NT, EXPERTS]), sb("eq", [P, NT, NE]), sb("oh", [P, NT, NE]), sb("pos3", [P, NT, NE])
        oh_bf = sb("oh_bf", [P, NT, NE], BF16)
        mx8, mx7, zs = sb("mx8", [P, NT]), sb("mx7", [P, NT]), sb("zs", [P, NT])
        p0, pm, g0 = sb("p0", [P, NT]), sb("pm", [P, NT]), sb("g0", [P, NT])
        eidx = sb("eidx", [P, NT, NE])
        tok = sb("tok", [P, NT])
        tot, carry, fresh = sb("tot", [P, NE, NT]), sb("carry", [P, NE, NT]), sb("fresh", [P, NE, NT])
        cnt, ntile, tends, tbase = (sb(n, [P, NE]) for n in ("cnt", "ntile", "tends", "tbase"))
        pos = sb("pos", [P, NT])
        pos_i = sb("pos_i", [P, NT], I32)
        tno = sb("tno", [P, TILES, NE])
        tcmp, texp = sb("tcmp", [P, TILES, NE]), sb("texp", [P, TILES])
        woff = sb("woff", [P, TILES], I32)
        xs = sb("xs", [P, 2, ROW])
        xsT = sb("xsT", [P, 2, P])
        hN = sb("hN", [P, 2, FF])
        hT = sb("hT", [P, 2, FF])
        ys = sb("ys", [P, TILES * ROW])
        gt = sb("gt", [P, TILES])
        ytok = sb("ytok", [P, TILES], I32)

        s_x, s_w, s_v, s_w13, s_w2, s_zero = (sem(n) for n in ("s_x", "s_w", "s_v", "s_w13", "s_w2", "s_zero"))
        c_ones, c_id, c_pool, c_dve = sem("c_ones"), sem("c_id"), sem("c_pool"), sem("c_dve")
        zeros_set = sem("zeros_set")
        wdt_mm, wdt_sb, bdt_sb = sem("wdt_mm"), sem("wdt_sb"), sem("bdt_sb")
        ln1_var, ln1_rstd, ln1_done, dstep = sem("ln1_var"), sem("ln1_rstd"), sem("ln1_done"), sem("dstep")
        xn_ready, xn_T, xnT_ready = sem("xn_ready"), sem("xn_T"), sem("xnT_ready")
        dt_mm, b_mm, c_mm = sem("dt_mm"), sem("b_mm"), sem("c_mm")
        pos_done, abs_done, exp_done, log_done = sem("pos_done"), sem("abs_done"), sem("exp_done"), sem("log_done")
        cont_done, cm_done, pstep, base_done = sem("cont_done"), sem("cm_done"), sem("pstep"), sem("base_done")
        att, nf_done, naf_done, sin_done, cos_done = sem("att"), sem("nf_done"), sem("naf_done"), sem("sin_done"), sem("cos_done")
        ret_done, y_mm, x2_done = sem("ret_done"), sem("y_mm"), sem("x2_done")
        ln2_var, ln2_rstd, xn2_done = sem("ln2_var"), sem("ln2_rstd"), sem("xn2_done")
        xn2_T, xn2T_ready, pay_done, lg_mm, lg_done = sem("xn2_T"), sem("xn2T_ready"), sem("pay_done"), sem("lg_mm"), sem("lg_done")
        h_mm, sil_done, h_done, y0_mm, y0_done = sem("h_mm"), sem("sil_done"), sem("h_done"), sem("y0_mm"), sem("y0_done")
        rt, rt_exp, oh_done, rank_mm, pos_ready, woff_ready = (sem(n) for n in ("rt", "rt_exp", "oh_done", "rank_mm", "pos_ready", "woff_ready"))
        z_ready, pay_gate, s_sort = sem("z_ready"), sem("pay_gate"), sem("s_sort")
        base_out, s_base = sem("base_out"), sem("s_base")
        s_xs = [sem("s_xs0"), sem("s_xs1")]
        xs_T, xsT_ready, dgate, dh1_mm, dh_mm, dsil, dh, dh_T, dhT, dy_mm, dy, dtok = (
            sem(n) for n in ("xs_T", "xsT_ready", "dgate", "dh1_mm", "dh_mm", "dsil", "dh", "dh_T", "dhT", "dy_mm", "dy", "dtok"))
        s_out = sem("s_out")

        def batch(t, b):
            return t[:, bass.ds(b * SEQ, SEQ)]

        def tiles(t, b):
            return t[:, bass.ds(b * TB, TB), :]

        def hold(eng):
            eng.wait_ge(c_id, 1)

        scr_tiles = scratch.rearrange("(t p) c -> t p c", p=P)

        block = ctx.enter_context(nc.Block())

        @block.sync
        def _(sp):
            for b in range(BATCH):
                sp.dma_start(xt[:, b * TB:(b + 1) * TB, :],
                             x[b * SEQ:(b + 1) * SEQ, :].rearrange("(j p) d -> p j d", p=P)).then_inc(s_x, 16)
            sp.dma_start(row[:], rows.partition_broadcast(P)).then_inc(s_v, 16)
            sp.dma_start(W1[:], w1t).then_inc(s_w13, 16)
            sp.dma_start(W3[:], w3t).then_inc(s_w13, 16)
            sp.dma_start(W2[:], w2t).then_inc(s_w2, 16)
            sp.wait_ge(zeros_set, 1)
            sp.dma_start(scratch.rearrange("(p t) c -> p (t c)", p=P), ys[:]).then_inc(s_zero, 16)
            sp.wait_ge(base_out, BATCH)
            sp.dma_start(out.rearrange("(j p) d -> p j d", p=P), y0[:]).then_inc(s_base, 16)

            def load_tile(t, q):
                sp.dma_start(xs[:, q, :], scr_tiles[t]).then_inc(s_xs[q], 16)

            sp.wait_ge(s_sort, 16 * NT)
            for t in range(2):
                load_tile(t, t)
            with sp.Fori(1, TILES // 2) as i:
                for q in range(2):
                    t = 2 * i + q
                    sp.wait_ge(xs_T, t - 1)
                    sp.wait_ge(dgate, t - 1)
                    sp.wait_ge(dtok, t - 1)
                    load_tile(t, q)

        @block.gpsimd
        def _(pool):
            pool.memset(ident[:], 0.0).then_inc(c_ones, 1)
            pool.memset(ones_bf[:], 1.0).then_inc(c_ones, 1)
            pool.memset(minus_half[:], -0.5).then_inc(c_ones, 1)
            pool.memset(one[:], 1.0).then_inc(c_ones, 1)
            pool.wait_ge(c_ones, 4)
            pool.affine_select(out=ident[:], in_=ident[:], compare_op=ALU.not_equal, fill=1.0, base=0,
                               pattern=[[-1, P]], channel_multiplier=1).then_inc(c_id, 1)
            pool.affine_select(out=tri[:], in_=ones_bf[:], compare_op=ALU.is_ge, fill=0.0, base=-1,
                               pattern=[[1, P]], channel_multiplier=-1).then_inc(c_pool, 1)
            pool.memset(half_pi[:], math.pi / 2).then_inc(c_pool, 1)
            pool.memset(ys[:], 0.0).then_inc(zeros_set, 1)
            pool.wait_ge(ln1_var, 1)
            pool.tensor_tensor(rstd[:], vpe[:], minus_half[:], ALU.pow).then_inc(ln1_rstd, 1)
            pool.iota(eidx[:], pattern=[[0, NT], [1, NE]], base=0, channel_multiplier=0,
                      allow_small_or_imprecise_dtypes=True).then_inc(c_pool, 1)
            pool.iota(tok[:], pattern=[[P, NT]], base=-TOKENS_OFF, channel_multiplier=1,
                      allow_small_or_imprecise_dtypes=True).then_inc(c_pool, 1)
            pool.iota(tno[:], pattern=[[1, TILES], [0, NE]], base=0, channel_multiplier=0,
                      allow_small_or_imprecise_dtypes=True).then_inc(c_pool, 1)
            pool.memset(fresh[:], 1.0).then_inc(c_pool, 1)
            pool.wait_ge(c_pool, 6)
            pool.memset(fresh[:, :, 0:1], 0.0).then_inc(c_pool, 1)
            pool.wait_ge(s_v, 16)
            with pool.Fori(0, BATCH) as b:
                hold(pool)
                pool.wait_ge(xn_ready, b + 1)
                flat = tiles(xt, b)
                pool.tensor_tensor(xnD[:], xn[:], row[:, 0:1, :].to_broadcast([P, TB, DIM]), ALU.mult).then_inc(pstep, 1)
                pool.tensor_tensor(flat, flat, row[:, 1:2, :].to_broadcast([P, TB, DIM]), ALU.add).then_inc(pstep, 1)
                pool.wait_ge(pstep, 2 * b + 2)
                pool.tensor_tensor(spare[:], minus_half[:, 0:1], minus_half[:, 0:1], ALU.mult)
                pool.tensor_tensor(flat, flat, xnD[:], ALU.add).then_inc(base_done, 1)
            with pool.Fori(0, BATCH) as b:
                pool.wait_ge(ln2_var, b + 1)
                pool.tensor_tensor(rstd[:, 0:TB], vpe[:, 0:TB], minus_half[:, 0:TB], ALU.pow).then_inc(ln2_rstd, 1)
            pool.wait_ge(pay_gate, 2)
            pool.wait_ge(pay_done, BATCH)
            pool.wait_ge(pos_ready, 1)
            pool.wait_ge(s_zero, 16)
            for j in range(NT):
                pool.indirect_dma_start(scratch, bass.IndirectOffsetOnAxis(pos_i[:, j:j + 1], 0),
                                        pay[:, j, :], None).then_inc(s_sort, 16)
            pool.wait_ge(s_base, 16)
            for t in range(TILES):
                pool.wait_ge(dtok, t + 1)
                pool.wait_ge(dy, t + 1)
                pool.indirect_dma_start(out, bass.IndirectOffsetOnAxis(ytok[:, t:t + 1], 0),
                                        ys[:, t * DIM:(t + 1) * DIM], None, bounds_check=TOKENS - 1,
                                        oob_is_err=False, compute_op=ALU.add).then_inc(s_out, 16)
            pool.wait_ge(s_out, 16 * TILES)

        @block.scalar
        def _(act):
            for dst, src in ((wd1t, w_dt1t), (wd2, w_dt2), (bd1, b_dt1), (vec, vecs), (wB, w_b), (wC, w_c),
                             (wO, w_out), (wR, w_rt)):
                act.dma_start(dst[:], src).then_inc(s_w, 16)
            act.wait_ge(wdt_mm, 1)
            act.activation(wdt[:], bank[1][:, 0:DIM], ACT.Copy).then_inc(wdt_sb, 1)

            with act.Fori(0, BATCH) as b:
                hold(act)
                act.wait_ge(xn_T, b + 1)
                act.activation(batch(xnT, b), bank[0][:], ACT.Copy).then_inc(xnT_ready, 1)
                act.wait_ge(dt_mm, b + 1)
                act.wait_ge(bdt_sb, 1)
                act.activation(r_abs[:], bank[1][:], ACT.Abs, bias=bdt[:, 0:1]).then_inc(abs_done, 1)
                hold(act)
                act.wait_ge(abs_done, b + 1)
                act.activation(batch(r_log, b), r_abs[:], ACT.Exp, scale=-1.0).then_inc(exp_done, 1)
                hold(act)
                act.wait_ge(c_mm, b + 1)
                act.activation(batch(CmT, b), bank[3][:], ACT.Identity, bias=vec[:, 1:2]).then_inc(cm_done, 1)
            with act.Fori(0, BATCH) as b:
                hold(act)
                act.wait_ge(exp_done, b + 1)
                act.activation(batch(r_log, b), batch(r_log, b), ACT.Ln, bias=1.0).then_inc(log_done, 1)

            def phase(b, first=False):
                act.wait_ge(nf_done, b + 1)
                if not first:
                    act.wait_ge(ret_done, b)
                act.activation(naf[:], nf[:], ACT.Abs).then_inc(naf_done, 1)
                act.activation(sn[:], nf[:], ACT.Sin, scale=-TWO_PI).then_inc(sin_done, 1)
                act.wait_ge(naf_done, b + 1)
                act.activation(cs[:], naf[:], ACT.Sin, scale=-TWO_PI, bias=half_pi[:, 0:1]).then_inc(cos_done, 1)

            def keep_norm(b, first=False):
                hold(act)
                act.wait_ge(xn2_done, b + 1)
                act.activation(tiles(pay, b)[:, :, 0:DIM], xn2[:], ACT.Copy).then_inc(pay_done, 1)
                act.wait_ge(xn2_T, b + 1)
                if not first:
                    act.wait_ge(h_mm, KF * b)
                act.activation(xn2T[:], bank[5][:], ACT.Copy).then_inc(xn2T_ready, 1)

            def silu0(b, k, first=False):
                act.wait_ge(h_mm, KF * b + k + 1)
                if not first or k >= 2:
                    act.wait_ge(h_done, KF * b + k - 1)
                act.activation(sil[:, k % 2, :], bank[2 * (k % 2)][:], ACT.Silu).then_inc(sil_done, 1)

            def keep_y0(b):
                hold(act)
                act.wait_ge(y0_mm, b + 1)
                act.activation(tiles(y0, b), bank[7][:].rearrange("p (j d) -> p j d", j=TB), ACT.Copy).then_inc(y0_done, 1)

            act.wait_ge(c_pool, 2)
            phase(0, True)
            keep_norm(0, True)
            silu0(0, 0, True)
            silu0(0, 1, True)
            phase(1)
            silu0(0, 2, True)
            silu0(0, 3, True)
            keep_y0(0)
            keep_norm(1)
            with act.Fori(1, BATCH - 1) as b:
                silu0(b, 0)
                silu0(b, 1)
                phase(b + 1)
                silu0(b, 2)
                silu0(b, 3)
                keep_y0(b)
                keep_norm(b + 1)
            act.wait_ge(z_ready, 1)
            act.activation(ex[:], ex[:], ACT.Exp).then_inc(rt_exp, 1)
            for k in range(KF):
                silu0(BATCH - 1, k)
            keep_y0(BATCH - 1)

            def turn_x(t, q, i, first=False):
                hold(act)
                act.wait_ge(xs_T, t + 1)
                act.wait_ge(s_xs[q], 16 * (i + 1))
                if not first:
                    act.wait_ge(dh_mm, t - 1)
                act.activation(xsT[:, q, :], bank[5][:, 0:P], ACT.Copy).then_inc(xsT_ready, 1)
                act.activation(gt[:, bass.ds(t, 1)], xs[:, q, DIM:DIM + 1], ACT.Copy).then_inc(dgate, 1)

            def silu(t, q, first=False):
                act.wait_ge(dh1_mm, t + 1)
                if not first:
                    act.wait_ge(dh, t - 1)
                act.activation(sil[:, q, :], bank[2 * q][:], ACT.Silu).then_inc(dsil, 1)

            def keep_y(t, q):
                hold(act)
                act.wait_ge(dy_mm, t + 1)
                act.wait_ge(dgate, t + 1)
                act.activation(ys[:, bass.ds(t * DIM, DIM)], bank[7][:, 0:DIM], ACT.Copy,
                               scale=gt[:, bass.ds(t, 1)]).then_inc(dy, 1)

            act.wait_ge(s_zero, 16)
            turn_x(0, 0, 0, True)
            turn_x(1, 1, 0, True)
            silu(0, 0, True)
            turn_x(2, 0, 1)
            silu(1, 1, True)
            keep_y(0, 0)
            with act.Fori(1, TILES // 2 - 1) as i:
                for q in range(2):
                    t = 2 * i + q
                    turn_x(t + 1, 1 - q, i + q)
                    silu(t, q)
                    keep_y(t - 1, 1 - q)
            t = TILES - 2
            turn_x(t + 1, 1, t // 2)
            silu(t, 0)
            keep_y(t - 1, 1)
            silu(t + 1, 1)
            keep_y(t, 0)
            keep_y(t + 1, 1)

        @block.tensor
        def _(pe):
            mm = pe.matmul
            pe.wait_ge(s_w, 16 * 8)
            mm(bank[1][:, 0:DIM], wd1t[:], wd2[:], start=True, stop=True)
            mm(bank[1][:, DIM:DIM + 1], wd2[:], bd1[:], start=True, stop=True).then_inc(wdt_mm, 1)
            pe.wait_ge(c_id, 1)
            pe.wait_ge(wdt_sb, 1)
            pe.wait_ge(bdt_sb, 1)

            def project(b, first=False):
                pe.wait_ge(xn_ready, b + 1)
                if not first:
                    pe.wait_ge(xnT_ready, b)
                for j in range(TB):
                    last = pe.transpose(bank[0][:, j * P:(j + 1) * P], xn[:, j, :], ident[:])
                last.then_inc(xn_T, 1)
                pe.wait_ge(xnT_ready, b + 1)
                if not first:
                    pe.wait_ge(abs_done, b)
                    pe.wait_ge(pos_done, b)
                mm(bank[1][:], wdt[:], batch(xnT, b), start=True, stop=True).then_inc(dt_mm, 1)
                if not first:
                    pe.wait_ge(cont_done, b)
                mm(bank[2][:], wB[:], batch(xnT, b), start=True, stop=True).then_inc(b_mm, 1)
                if not first:
                    pe.wait_ge(cm_done, b)
                mm(bank[3][:], wC[:], batch(xnT, b), start=True, stop=True).then_inc(c_mm, 1)

            project(0, True)
            with pe.Fori(1, BATCH) as b:
                project(b)

            def out_proj(b, first=False):
                pe.wait_ge(ret_done, b + 1)
                if not first:
                    pe.wait_ge(x2_done, b)
                for j in range(TB):
                    last = mm(bank[4][:, j * DIM:(j + 1) * DIM], ret[:, j * P:(j + 1) * P], wO[:], start=True, stop=True)
                last.then_inc(y_mm, 1)

            def turn2(b, first=False):
                pe.wait_ge(xn2_done, b + 1)
                if not first:
                    pe.wait_ge(xn2T_ready, b)
                for j in range(TB):
                    last = pe.transpose(bank[5][:, j * P:(j + 1) * P], xn2[:, j, :], ident[:])
                last.then_inc(xn2_T, 1)

            def logits(b, first=False):
                pe.wait_ge(xn2T_ready, b + 1)
                if not first:
                    pe.wait_ge(lg_done, b)
                for j in range(TB):
                    last = mm(bank[6][:, j * EXPERTS:(j + 1) * EXPERTS], xn2T[:, j * P:(j + 1) * P], wR[:], start=True, stop=True)
                last.then_inc(lg_mm, 1)

            def hidden0(b, k, first=False):
                if not first or k >= 2:
                    pe.wait_ge(h_done, KF * b + k - 1)
                pair = 2 * (k % 2)
                mm(bank[pair][:], W1[:, k * P:(k + 1) * P], xn2T[:], start=True, stop=True)
                mm(bank[pair + 1][:], W3[:, k * P:(k + 1) * P], xn2T[:], start=True, stop=True).then_inc(h_mm, 1)

            def down0(b, first=False):
                pe.wait_ge(h_done, KF * (b + 1))
                if not first:
                    pe.wait_ge(y0_done, b)
                for j in range(TB):
                    for k in range(KF):
                        last = mm(bank[7][:, j * DIM:(j + 1) * DIM], hT0[:, k, j * P:(j + 1) * P],
                                  W2[:, k * DIM:(k + 1) * DIM], start=(k == 0), stop=(k == KF - 1))
                last.then_inc(y0_mm, 1)

            def steady(b, first=False):
                for k in range(3):
                    hidden0(b, k, first)
                out_proj(b + 1)
                hidden0(b, 3, first)
                turn2(b + 1)
                down0(b, first)
                logits(b + 1)

            out_proj(0, True)
            turn2(0, True)
            logits(0, True)
            pe.wait_ge(s_w13, 32)
            pe.wait_ge(s_w2, 16)
            pe.wait_ge(pos_done, BATCH)
            pe.wait_ge(cont_done, BATCH)
            pe.wait_ge(cm_done, BATCH)
            steady(0, True)
            with pe.Fori(1, BATCH - 1) as b:
                steady(b)
            hidden0(BATCH - 1, 0)
            hidden0(BATCH - 1, 1)
            pe.wait_ge(oh_done, 1)
            pe.wait_ge(lg_done, BATCH)
            flat = oh_bf[:].rearrange("p j e -> p (j e)")
            mm(bank[6][:, 0:NT * NE], tri[:], flat, start=True, stop=True)
            mm(bank[6][:, NT * NE:2 * NT * NE], ones_bf[:], flat, start=True, stop=True).then_inc(rank_mm, 1)
            hidden0(BATCH - 1, 2)
            hidden0(BATCH - 1, 3)
            down0(BATCH - 1)

            def turn_x(t, q, i, first=False):
                pe.wait_ge(s_xs[q], 16 * (i + 1))
                if not first:
                    pe.wait_ge(xsT_ready, t)
                pe.transpose(bank[5][:, 0:P], xs[:, q, 0:DIM], ident[:]).then_inc(xs_T, 1)

            def up(bk, w, off, t, q):
                return mm(bank[bk][:], xsT[:, q, :], w[:, bass.ds(off, FF)], start=True, stop=True)

            def offset(t):
                return pe.value_load(woff[0:1, bass.ds(t, 1)], min_val=FF, max_val=(EXPERTS - 1) * FF)

            def turn_h(t, q, first=False):
                pe.wait_ge(dh, t + 1)
                if not first:
                    pe.wait_ge(dhT, t - 1)
                for k in range(KF):
                    last = pe.transpose(bank[4 + 2 * q][:, k * P:(k + 1) * P], hN[:, q, k * P:(k + 1) * P], ident[:])
                last.then_inc(dh_T, 1)

            def down(t, q, off, first=False):
                pe.wait_ge(dhT, t + 1)
                if not first:
                    pe.wait_ge(dy, t)
                for k in range(KF):
                    last = mm(bank[7][:, 0:DIM], hT[:, q, k * P:(k + 1) * P],
                              W2[:, bass.ds(off + k * DIM, DIM)], start=(k == 0), stop=(k == KF - 1))
                last.then_inc(dy_mm, 1)

            def tile_step(t, q, i_next, more=True, first=False, second=False):
                if more:
                    turn_x(t + 1, 1 - q, i_next)
                off = offset(t)
                pe.wait_ge(xsT_ready, t + 1)
                if not (first or second):
                    pe.wait_ge(dh, t - 1)
                up(2 * q, W1, off, t, q).then_inc(dh1_mm, 1)
                if not first:
                    turn_h(t - 1, 1 - q, second)
                up(2 * q + 1, W3, off, t, q).then_inc(dh_mm, 1)
                if not first:
                    down(t - 1, 1 - q, offset(t - 1), second)

            pe.wait_ge(woff_ready, 1)
            turn_x(0, 0, 0, True)
            pe.wait_ge(y0_done, BATCH)
            tile_step(0, 0, 0, first=True)
            tile_step(1, 1, 1, second=True)
            tile_step(2, 0, 1)
            with pe.Fori(1, TILES // 2 - 1) as i:
                tile_step(2 * i + 1, 1, i + 1)
                tile_step(2 * i + 2, 0, i + 1)
            t = TILES - 1
            tile_step(t, 1, 0, more=False)
            turn_h(t, 1)
            down(t, 1, offset(t))

        @block.vector
        def _(dve):
            count = [0]

            def link(ins):
                count[0] += 1
                ins.then_inc(dstep, 1)
                dve.wait_ge(dstep, count[0])

            def statistics(n, step):
                half = [st[:, 0:n, c:c + 1].rearrange("p n o -> p (n o)") for c in (1, 2, 4, 5)]
                step(dve.tensor_tensor(t_a[:, 0:n], half[0], half[2], ALU.add))
                step(dve.tensor_tensor(t_b[:, 0:n], half[0], half[2], ALU.subtract))
                step(dve.tensor_tensor(t_c[:, 0:n], half[1], half[3], ALU.add))
                step(dve.tensor_tensor(t_b[:, 0:n], t_b[:, 0:n], t_b[:, 0:n], ALU.mult))
                step(dve.tensor_scalar(mean[:, 0:n], t_a[:, 0:n], 0.5, None, ALU.mult))
                step(dve.tensor_scalar(t_c[:, 0:n], t_c[:, 0:n], 1.0 / DIM, EPS, ALU.mult, ALU.add))
                return dve.scalar_tensor_tensor(out=vpe[:, 0:n], in0=t_b[:, 0:n], scalar=0.25, in1=t_c[:, 0:n],
                                                op0=ALU.mult, op1=ALU.add)

            dve.wait_ge(s_x, 16 * BATCH)
            with dve.Fori(0, BATCH) as b:
                for j in range(TB):
                    last = dve.bn_stats(st[:, bass.ds(b * TB + j, 1), :], xt[:, bass.ds(b * TB + j, 1), :])
                last.then_inc(ln1_done, 1)
            dve.wait_ge(ln1_done, BATCH)
            statistics(NT, link).then_inc(ln1_var, 1)
            dve.wait_ge(wdt_sb, 1)
            dve.tensor_tensor(bdt[:], bank[1][:, DIM:DIM + 1], vec[:, 2:3], ALU.add).then_inc(bdt_sb, 1)
            dve.tensor_scalar(turn[:], vec[:, 3:4], 1.0 / (2.0 * math.pi), None, ALU.mult).then_inc(c_dve, 1)
            dve.wait_ge(ln1_rstd, 1)

            def normalise(b, first=False):
                if not first:
                    dve.wait_ge(xn_T, b)
                    dve.wait_ge(base_done, b)
                for j in range(TB):
                    at = bass.ds(b * TB + j, 1)
                    last = dve.tensor_scalar(xn[:, j, :], xt[:, at, :].rearrange("p o d -> p (o d)"), mean[:, at], rstd[:, at],
                                             ALU.subtract, ALU.mult)
                last.then_inc(xn_ready, 1)

            def contents(b):
                dve.wait_ge(abs_done, b + 1)
                dve.tensor_scalar(batch(r_pos, b), bank[1][:], bdt[:, 0:1], 0.0, ALU.add, ALU.max).then_inc(pos_done, 1)
                dve.wait_ge(b_mm, b + 1)
                dve.scalar_tensor_tensor(out=batch(cont, b), in0=bank[2][:], scalar=vec[:, 0:1], in1=batch(xnT, b),
                                         op0=ALU.add, op1=ALU.mult).then_inc(cont_done, 1)

            normalise(0, True)
            with dve.Fori(1, BATCH) as b:
                normalise(b)
                contents(b - 1)
            contents(BATCH - 1)

            STEPS = 16

            def steps(b):
                n = [0]

                def step(ins):
                    n[0] += 1
                    ins.then_inc(att, 1)
                    dve.wait_ge(att, STEPS * b + n[0])
                return step, n

            def phases(b, step, first=False):
                dve.wait_ge(log_done, b + 1)
                step(dve.tensor_tensor_scan(cum[:], batch(r_pos, b), batch(r_log, b), 0.0, ALU.add, ALU.add))
                dve.tensor_scalar(tph[:], cum[:], turn[:, 0:1], None, ALU.mult)
                step(dve.tensor_scalar(kph[:], cum[:], turn[:, 0:1], MAGIC, ALU.mult, ALU.add))
                if not first:
                    dve.wait_ge(sin_done, b)
                    dve.wait_ge(naf_done, b)
                dve.scalar_tensor_tensor(out=nf[:], in0=kph[:], scalar=MAGIC, in1=tph[:],
                                         op0=ALU.subtract, op1=ALU.subtract).then_inc(nf_done, 1)

            def memory(b, step):
                dve.wait_ge(sin_done, b + 1)
                step(dve.tensor_tensor(csn[:], batch(cont, b), sn[:], ALU.mult))
                step(dve.tensor_tensor_scan(mi[:], one[:], csn[:], 0.0, ALU.mult, ALU.add))
                dve.wait_ge(cos_done, b + 1)
                step(dve.tensor_tensor(cc[:], batch(cont, b), cs[:], ALU.mult))
                step(dve.tensor_tensor_scan(mr[:], one[:], cc[:], 0.0, ALU.mult, ALU.add))

            def retrieve(b, step, first=False):
                step(dve.tensor_tensor(csn[:], mi[:], sn[:], ALU.mult))
                step(dve.tensor_tensor(cc[:], mr[:], cs[:], ALU.mult))
                step(dve.tensor_tensor(mr[:], cc[:], csn[:], ALU.add))
                dve.wait_ge(cm_done, b + 1)
                if not first:
                    dve.wait_ge(y_mm, b)
                dve.tensor_tensor(ret[:], mr[:], batch(CmT, b), ALU.mult).then_inc(ret_done, 1)

            def residual(b, step, first=False):
                dve.wait_ge(y_mm, b + 1)
                dve.wait_ge(base_done, b + 1)
                dve.tensor_tensor(tiles(x2, b), bank[4][:].rearrange("p (j d) -> p j d", j=TB), tiles(xt, b),
                                  ALU.add).then_inc(x2_done, 1)
                hold(dve)
                dve.wait_ge(x2_done, b + 1)
                for j in range(TB):
                    last = dve.bn_stats(st[:, j:j + 1, :], x2[:, bass.ds(b * TB + j, 1), :])
                step(last)
                statistics(TB, step).then_inc(ln2_var, 1)
                dve.wait_ge(ln2_rstd, b + 1)
                if not first:
                    dve.wait_ge(xn2_T, b)
                    dve.wait_ge(pay_done, b)
                for j in range(TB):
                    at = bass.ds(b * TB + j, 1)
                    last = dve.tensor_scalar(xn2[:, j, :], x2[:, at, :].rearrange("p o d -> p (o d)"), mean[:, j:j + 1],
                                             rstd[:, j:j + 1], ALU.subtract, ALU.mult)
                last.then_inc(xn2_done, 1)

            def keep_logits(b):
                dve.wait_ge(lg_mm, b + 1)
                dve.tensor_copy(tiles(lg, b), bank[6][:, 0:TB * EXPERTS].rearrange("p (j e) -> p j e", j=TB)).then_inc(lg_done, 1)

            def hidden0(b, k, first=False):
                dve.wait_ge(sil_done, KF * b + k + 1)
                if not first and k == 0:
                    dve.wait_ge(y0_mm, b)
                dve.tensor_tensor(hT0[:, k, :], sil[:, k % 2, :], bank[2 * (k % 2) + 1][:], ALU.mult).then_inc(h_done, 1)

            def steady(b, first=False):
                step, n = steps(b + 1)
                phases(b + 1, step)
                hidden0(b, 0, first)
                memory(b + 1, step)
                hidden0(b, 1, first)
                retrieve(b + 1, step)
                hidden0(b, 2, first)
                hidden0(b, 3, first)
                residual(b + 1, step)
                keep_logits(b + 1)
                assert n[0] <= STEPS
                for _ in range(STEPS - n[0]):
                    dve.sem_inc(att, 1)

            dve.wait_ge(c_dve, 1)
            dve.wait_ge(c_ones, 4)
            step, n = steps(0)
            phases(0, step, True)
            memory(0, step)
            retrieve(0, step, True)
            residual(0, step, True)
            keep_logits(0)
            STEPS_USED = n[0]
            assert STEPS_USED == STEPS, STEPS_USED
            steady(0, True)
            with dve.Fori(1, BATCH - 1) as b:
                steady(b)

            def over(t, n):
                return t[:].rearrange("p (j o) -> p j o", o=1).to_broadcast([P, NT, n])

            dve.wait_ge(lg_done, BATCH)
            dve.wait_ge(c_pool, 7)
            chosen = lg[:, :, 1:EXPERTS]
            dve.tensor_reduce(mx8[:], lg[:], AX.X, ALU.max)
            link(dve.tensor_reduce(mx7[:], chosen, AX.X, ALU.max))
            dve.tensor_tensor(ex[:], lg[:], over(mx8, EXPERTS), ALU.subtract).then_inc(z_ready, 1)
            link(dve.tensor_tensor(eq[:], chosen, over(mx7, NE), ALU.is_equal))
            link(dve.scalar_tensor_tensor(out=eq[:], in0=eq[:], scalar=-16.0, in1=eidx[:], op0=ALU.mult, op1=ALU.add))
            link(dve.tensor_reduce(zs[:], eq[:], AX.X, ALU.min))
            link(dve.tensor_tensor(oh[:], eq[:], over(zs, NE), ALU.is_equal))
            dve.tensor_copy(oh_bf[:], oh[:]).then_inc(oh_done, 1)
            hidden0(BATCH - 1, 0)
            dve.wait_ge(rank_mm, 1)
            nn = NT * NE
            ranks = bank[6][:, 0:nn].rearrange("p (j e) -> p j e", e=NE)
            link(dve.tensor_copy(tot[:], bank[6][:, nn:2 * nn].rearrange("p (j e) -> p e j", e=NE)))
            flat = [t[:].rearrange("p e j -> p (e j)") for t in (carry, fresh, tot)]
            link(dve.tensor_tensor_scan(flat[0], flat[1], flat[2], 0.0, ALU.mult, ALU.add))
            link(dve.tensor_tensor(carry[:], carry[:], tot[:], ALU.subtract))
            link(dve.tensor_reduce(cnt[:], tot[:], AX.X, ALU.add))
            link(dve.tensor_scalar(ntile[:], cnt[:], 1.0 / P, (P - 1.0) / P - 0.5 + 0.5 / P, ALU.mult, ALU.add))
            link(dve.tensor_scalar(ntile[:], ntile[:], MAGIC, None, ALU.add))
            link(dve.tensor_scalar(ntile[:], ntile[:], MAGIC, None, ALU.subtract))
            link(dve.tensor_tensor_scan(tends[:], one[:, 0:NE], ntile[:], 0.0, ALU.mult, ALU.add))
            link(dve.tensor_tensor(tbase[:], tends[:], ntile[:], ALU.subtract))
            link(dve.tensor_tensor(pos3[:], ranks, carry[:].rearrange("p e j -> p j e"), ALU.add))
            base = tbase[:].rearrange("p (o e) -> p o e", o=1).to_broadcast([P, NT, NE])
            link(dve.scalar_tensor_tensor(out=pos3[:], in0=base, scalar=float(P), in1=pos3[:], op0=ALU.mult, op1=ALU.add))
            link(dve.tensor_tensor(pos3[:], pos3[:], oh[:], ALU.mult))
            link(dve.tensor_reduce(pos[:], pos3[:], AX.X, ALU.add))
            dve.tensor_copy(pos_i[:], pos[:]).then_inc(pos_ready, 1)
            dve.wait_ge(rt_exp, 1)
            link(dve.tensor_reduce(zs[:], ex[:], AX.X, ALU.add))
            link(dve.reciprocal(zs[:], zs[:]))
            link(dve.tensor_reduce(pm[:], ex[:, :, 1:EXPERTS], AX.X, ALU.max))
            link(dve.tensor_tensor(pm[:], pm[:], zs[:], ALU.mult))
            link(dve.tensor_tensor(p0[:], ex[:, :, 0:1].rearrange("p j o -> p (j o)"), zs[:], ALU.mult))
            link(dve.tensor_tensor(zs[:], p0[:], pm[:], ALU.add))
            link(dve.tensor_scalar(zs[:], zs[:], 1e-9, None, ALU.max))
            link(dve.reciprocal(zs[:], zs[:]))
            dve.wait_ge(pay_done, BATCH)
            dve.tensor_tensor(pay[:, :, DIM:DIM + 1].rearrange("p j o -> p (j o)"), pm[:], zs[:], ALU.mult).then_inc(pay_gate, 1)
            dve.tensor_copy(pay[:, :, DIM + 1:DIM + 2].rearrange("p j o -> p (j o)"), tok[:]).then_inc(pay_gate, 1)
            link(dve.tensor_tensor(g0[:], p0[:], zs[:], ALU.mult))
            ends = tends[:].rearrange("p (o e) -> p o e", o=1).to_broadcast([P, TILES, NE])
            link(dve.tensor_tensor(tcmp[:], tno[:], ends, ALU.is_ge))
            link(dve.tensor_reduce(texp[:], tcmp[:], AX.X, ALU.add))
            link(dve.tensor_scalar(texp[:], texp[:], NE - 1.0, 1.0, ALU.min, ALU.add))
            dve.tensor_scalar(woff[:], texp[:], float(FF), None, ALU.mult).then_inc(woff_ready, 1)
            for k in range(1, KF):
                hidden0(BATCH - 1, k)
            dve.wait_ge(y0_done, BATCH)
            with dve.Fori(0, BATCH) as b:
                for j in range(TB):
                    at = bass.ds(b * TB + j, 1)
                    row_of = [t[:, at, :].rearrange("p o d -> p (o d)") for t in (y0, x2)]
                    last = dve.scalar_tensor_tensor(out=row_of[0], in0=row_of[0], scalar=g0[:, at], in1=row_of[1],
                                                    op0=ALU.mult, op1=ALU.add)
                last.then_inc(base_out, 1)

            def token(t, q, i):
                dve.wait_ge(s_xs[q], 16 * (i + 1))
                dve.tensor_scalar(ytok[:, bass.ds(t, 1)], xs[:, q, DIM + 1:DIM + 2], float(TOKENS_OFF), None,
                                  ALU.add).then_inc(dtok, 1)

            def keep_hT(t, q, first=False):
                dve.wait_ge(dh_T, t + 1)
                if not first:
                    dve.wait_ge(dy_mm, t - 1)
                dve.tensor_copy(hT[:, q, :], bank[4 + 2 * q][:]).then_inc(dhT, 1)

            def hidden(t, q, first=False):
                dve.wait_ge(dsil, t + 1)
                dve.wait_ge(dh_mm, t + 1)
                if not first:
                    dve.wait_ge(dh_T, t - 1)
                dve.tensor_tensor(hN[:, q, :], sil[:, q, :], bank[2 * q + 1][:], ALU.mult).then_inc(dh, 1)

            token(0, 0, 0)
            token(1, 1, 0)
            hidden(0, 0, True)
            token(2, 0, 1)
            keep_hT(0, 0, True)
            hidden(1, 1, True)
            with dve.Fori(1, TILES // 2 - 1) as i:
                for q in range(2):
                    t = 2 * i + q
                    token(t + 1, 1 - q, i + q)
                    if q == 0:
                        keep_hT(t - 1, 1, False)
                    else:
                        keep_hT(t - 1, 0)
                    hidden(t, q)
            t = TILES - 2
            token(t + 1, 1, t // 2)
            keep_hT(t - 1, 1)
            hidden(t, 0)
            keep_hT(t, 0)
            hidden(t + 1, 1)
            keep_hT(t + 1, 1)


_OUT = (BATCH, SEQ, DIM)


def kernel(**a):
    import concourse.bacc as _bacc
    from concourse.bass_utils import run_bass_kernel_spmd as _run

    def col(v):
        return np.ascontiguousarray(np.asarray(v).reshape(-1, 1))

    w1, w2, w3 = (np.asarray(a["L0_ffn_" + n]) for n in ("W1", "W2", "W3"))
    put = {
        "x": np.asarray(a["L0_attn_x"]).reshape(TOKENS, DIM),
        "vecs": np.concatenate([col(a["L0_attn_" + n]) for n in ("b_B", "b_C", "b_dt2", "omega_base")], axis=1),
        "b_dt1": col(a["L0_attn_b_dt1"]),
        "rows": np.stack([np.asarray(a["L0_attn_D"]), np.asarray(a["L0_attn_b_out"])]),
        "w_b": np.asarray(a["L0_attn_W_B"]),
        "w_c": np.asarray(a["L0_attn_W_C"]),
        "w_dt1t": np.asarray(a["L0_attn_W_dt1"]).T,
        "w_dt2": np.asarray(a["L0_attn_W_dt2"]),
        "w_out": np.asarray(a["L0_attn_W_out"]),
        "w_rt": np.asarray(a["L0_ffn_Wr"]).T,
        "w1t": w1.transpose(2, 0, 1).reshape(DIM, EXPERTS * FF),
        "w3t": w3.transpose(2, 0, 1).reshape(DIM, EXPERTS * FF),
        "w2t": w2.reshape(EXPERTS, DIM, KF, P).transpose(3, 0, 2, 1).reshape(P, EXPERTS * FF),
    }
    nc = _bacc.Bacc("TRN2", target_bir_lowering=False, num_devices=1)
    arrays, args = {}, []
    for name, v in put.items():
        v = np.ascontiguousarray(v)
        arrays[name + "_in"] = v
        args.append(nc.dram_tensor(name + "_in", v.shape, mybir.dt.from_np(v.dtype), kind="ExternalInput").ap())
    out = nc.dram_tensor("out_0", [TOKENS, DIM], F32, kind="ExternalOutput").ap()
    scratch = nc.dram_tensor("sorted_rows", [SLOTS, ROW], F32, kind="Internal").ap()
    build(nc, *args, out, scratch)
    r = _run(nc, [arrays], core_ids=[0])
    return r.results[0]["out_0"].reshape(_OUT)
```

```python
from contextlib import ExitStack
import math

import numpy as np

import concourse.bass as bass
from concourse import mybir

P = 128
F32 = mybir.dt.float32
F32R = mybir.dt.float32r
BF16 = mybir.dt.bfloat16
I32 = mybir.dt.int32
U32 = mybir.dt.uint32
ALU = mybir.AluOpType
ACT = mybir.ActivationFunctionType
AX = mybir.AxisListType

BATCH, SEQ, DIM, DT_RANK = 4, 512, 128, 32
TOKENS = BATCH * SEQ
NT = TOKENS // P
TB = SEQ // P
EXPERTS, FF = 8, 512
NE = EXPERTS - 1
KF = FF // P
TILES = (TOKENS + NE * (P - 1)) // P
REGION = NT
TAIL = TILES - TOKENS // P
SORTED = NE * REGION + TAIL
ROW = DIM + 2
TOKENS_OFF = 2 * TOKENS
EPS = 1e-5
SET_LN_EXP, SET_SILU_SIN = 6, 18
MAGIC = 1.5 * 2.0 ** 23
UNROLL = 6
ZROWS = 2
TWO_PI = 6.283185


def build(nc, x, rows, w_dt, w_att, w_ff, out, scratch):
    with ExitStack() as ctx:
        def sb(name, shape, dt=F32):
            return ctx.enter_context(nc.sbuf_tensor(name, shape, dt))

        def sem(name):
            return ctx.enter_context(nc.semaphore(name))

        bank = [ctx.enter_context(nc.psum_tensor(f"bank{i}", [P, 512], F32)) for i in range(8)]

        wd = sb("wd", [DT_RANK, 2 * DIM + 1])
        wd1t, wd2, bd1 = wd[:, 0:DIM], wd[:, DIM:2 * DIM], wd[:, 2 * DIM:2 * DIM + 1]
        wdt, bdt = sb("wdt", [P, DIM]), sb("bdt", [P, 1])
        wa = sb("wa", [P, 3 * DIM + EXPERTS + 4])
        wB, wC, wO = (wa[:, n * DIM:(n + 1) * DIM] for n in range(3))
        wR = wa[:, 3 * DIM:3 * DIM + EXPERTS]
        vec = wa[:, 3 * DIM + EXPERTS:]
        w_e0 = sb("w_e0", [P, 3 * FF])
        stage = sb("stage", [P, 2, 3 * FF])
        turn = sb("turn", [P, 1])
        RANKS_AT = TB * EXPERTS
        half_pi = sb("half_pi", [P, 1])
        row = sb("row", [P, 2, DIM])
        ident = sb("ident", [P, P])
        tri = sb("tri", [P, P], BF16)
        ones_bf = sb("ones_bf", [P, P], BF16)
        zrow = sb("zrow", [P, ZROWS * ROW])
        minus_half = sb("minus_half", [P, NT])
        xt = sb("xt", [P, NT, DIM])
        st = sb("st", [P, NT, 6])
        mv = sb("mv", [P, NT, 2])
        rstd, vpe = sb("rstd", [P, NT]), sb("vpe", [P, NT])
        xn = sb("xn", [P, NT, DIM])
        xnD = sb("xnD", [P, 2, TB, DIM])
        xnT = sb("xnT", [P, TOKENS])
        one = sb("one", [P, SEQ])
        x2 = xt
        xn2 = sb("xn2", [P, TB, DIM])
        xn2T = xn[:].rearrange("p j d -> p (j d)")
        xn2S = sb("xn2S", [P, SEQ])
        pay = sb("pay", [P, NT, ROW])
        sil = sb("sil", [P, 2, FF])
        hT0 = sb("hT0", [P, KF, SEQ])
        y0T = sb("y0T", [P, SEQ])
        y0 = xnT[:].rearrange("p (j d) -> p j d", d=DIM)
        ex = sb("ex", [P, NT, EXPERTS + 1])
        eq, pos3 = sb("eq", [P, TB, NE]), sb("pos3", [P, TB, NE])
        oh = sb("oh", [P, NT, NE], BF16)
        seen = sb("seen", [P, NE], BF16)
        seen_b = sb("seen_b", [P, NE])
        mx8, mx7, mn = sb("mx8", [P, TB]), sb("mx7", [P, TB]), sb("mn", [P, TB])
        zs, pr, gs = sb("zs", [P, TB]), sb("pr", [P, TB, 2]), sb("gs", [P, TB])
        g0 = sb("g0", [P, NT])
        eidx = sb("eidx", [P, TB, NE])
        starts, magic_starts = sb("starts", [P, NE]), sb("magic_starts", [P, NE])
        ntile, spare_tiles, tends = (sb(n, [P, NE]) for n in ("ntile", "spare_tiles", "tends"))
        pos = sb("pos", [P, TB])
        pos_i = sb("pos_i", [P, NT], I32)
        tno = sb("tno", [P, TILES, NE])
        tcmp, texp, tskip = sb("tcmp", [P, TILES, NE]), sb("texp", [P, TILES]), sb("tskip", [P, TILES])
        expert_of = sb("expert_of", [P, TILES], I32)
        place_of = sb("place_of", [P, TILES], I32)
        gt = sb("gt", [P, TILES])
        ytok = sb("ytok", [P, TILES], I32)

        SPLIT = 2 * 3 * FF
        HELD = 5
        with ExitStack() as early:
            def eb(name, shape, dt=F32):
                return early.enter_context(nc.sbuf_tensor(name, shape, dt))

            eb("held", [P, HELD * SPLIT])
            r_pos = eb("r_pos", [P, TOKENS])
            r_log = eb("r_log", [P, TOKENS])
            r_abs, cum, kph, tph = (eb(n, [P, SEQ]) for n in ("r_abs", "cum", "kph", "tph"))
            nf, naf, mr, mi, mis, ret = (eb(n, [P, SEQ]) for n in ("nf", "naf", "mr", "mi", "mis", "ret"))
            sn, cs, cc, csn = ([eb(n + str(q), [P, SEQ]) for q in range(2)] for n in ("sn", "cs", "cc", "csn"))
            cont = eb("cont", [P, TOKENS])
        wx = sb("wx", [P, NE, 3 * KF, 2, P], F32R)
        xs = sb("xs", [P, 2, ROW])
        xh, xl = sb("xh", [P, 2, P], F32R), sb("xl", [P, 2, P], F32R)
        hN = sb("hN", [P, 2, FF])
        hh, hl = sb("hh", [P, 2, FF], F32R), sb("hl", [P, 2, FF], F32R)
        ys = sb("ys", [P, TILES * DIM])

        s_xb = [sem(f"s_x{b}") for b in range(BATCH)]
        s_w, s_wd, s_v, s_e0, s_zero, w_hi = (sem(n) for n in ("s_w", "s_wd", "s_v", "s_e0", "s_zero", "w_hi"))
        w_lo = [sem(f"w_lo{e}") for e in range(1, EXPERTS)]
        s_st = [sem("s_st0"), sem("s_st1")]
        c_ones, c_id, c_pool, c_dve = sem("c_ones"), sem("c_id"), sem("c_pool"), sem("c_dve")
        zeros_set, seen_set, tok_set = sem("zeros_set"), sem("seen_set"), sem("tok_set")
        wdt_mm, wdt_sb, bdt_sb = sem("wdt_mm"), sem("wdt_sb"), sem("bdt_sb")
        ln1_var, ln1_rstd, dstep = sem("ln1_var"), sem("ln1_rstd"), sem("dstep")
        xn_ready, xn_T, xnT_ready = sem("xn_ready"), sem("xn_T"), sem("xnT_ready")
        dt_mm, b_mm, c_mm = sem("dt_mm"), sem("b_mm"), sem("c_mm")
        pos_done, abs_done, exp_done, log_done = sem("pos_done"), sem("abs_done"), sem("exp_done"), sem("log_done")
        cont_done, pstep, base_done = sem("cont_done"), sem("pstep"), sem("base_done")
        csn_done, cc_done, mi_done, mis_done = sem("csn_done"), sem("cc_done"), sem("mi_done"), sem("mis_done")
        nf_done, naf_done, sin_done, cos_done = sem("nf_done"), sem("naf_done"), sem("sin_done"), sem("cos_done")
        ret_done, y_mm, x2_done = sem("ret_done"), sem("y_mm"), sem("x2_done")
        ln2_var, ln2_rstd, xn2_done = sem("ln2_var"), sem("ln2_rstd"), sem("xn2_done")
        xn2S_ready = sem("xn2S_ready")
        xn2_T, xn2T_ready, pay_done, lg_mm = sem("xn2_T"), sem("xn2T_ready"), sem("pay_done"), sem("lg_mm")
        h_mm, sil_done, h_done, down0_mm = sem("h_mm"), sem("sil_done"), sem("h_done"), sem("down0_mm")
        y0T_ready, y0_T = sem("y0T_ready"), sem("y0_T")
        rt_exp, oh_done, seen_done, rank_mm, rank_read, pos_ready = (
            sem(n) for n in ("rt_exp", "oh_done", "seen_done", "rank_mm", "rank_read", "pos_ready"))
        experts_ready, places_ready = sem("experts_ready"), sem("places_ready")
        z_ready, pay_gate, s_sort = sem("z_ready"), sem("pay_gate"), sem("s_sort")
        base_out, s_base, s_base_last = sem("base_out"), sem("s_base"), sem("s_base_last")
        s_xs = [sem("s_xs0"), sem("s_xs1")]
        xs_T, xh_ready, xl_ready, hh_ready, dgate, dh1_mm, dh_mm, dsil, dh, dh_T, hl_ready, dy_mm, dy_high, dy, dtok = (
            sem(n) for n in ("xs_T", "xh_ready", "xl_ready", "hh_ready", "dgate", "dh1_mm", "dh_mm", "dsil", "dh", "dh_T", "hl_ready", "dy_mm", "dy_high", "dy", "dtok"))
        s_out = sem("s_out")

        def batch(t, b):
            return t[:, bass.ds(b * SEQ, SEQ)]

        def tiles(t, b):
            return t[:, bass.ds(b * TB, TB), :]

        def hold(eng):
            eng.wait_ge(c_id, 1)

        def store_base(eng, b, stored):
            eng.wait_ge(base_out, b + 1)
            eng.dma_start(out[b * SEQ:(b + 1) * SEQ, :].rearrange("(j p) d -> p j d", p=P), tiles(y0, b)).then_inc(stored, 16)

        def low_parts(eng, e):
            eng.wait_ge(w_hi, e)
            whole = stage[:, (e - 1) % 2, :].rearrange("p (c n) -> p c n", n=P)
            eng.tensor_tensor(wx[:, e - 1, :, 1, :], whole, wx[:, e - 1, :, 0, :].bitcast(F32),
                              ALU.subtract).then_inc(w_lo[e - 1], 1)

        scr_tiles = scratch.rearrange("(t p) c -> t p c", p=P)

        DT_BANK, B_BANK, DOWN0_BANK = (1, 2, 3, 5), (6, 7, 1, 2), (7, 7, 7, 4)

        block = ctx.enter_context(nc.Block())

        @block.sync
        def _(sp):
            for b in range(BATCH):
                sp.dma_start(xt[:, b * TB:(b + 1) * TB, :],
                             x[b * SEQ:(b + 1) * SEQ, :].rearrange("(j p) d -> p j d", p=P)).then_inc(s_xb[b], 16)
            sp.dma_start(row[:], rows.partition_broadcast(P)).then_inc(s_v, 16)
            sp.wait_ge(s_w, 16)
            sp.dma_start(w_e0[:], w_ff[:, 0:3 * FF]).then_inc(s_e0, 16)

            def load_expert(e):
                sp.dma_start(stage[:, (e - 1) % 2, :], w_ff[:, e * 3 * FF:(e + 1) * 3 * FF]).then_inc(s_st[(e - 1) % 2], 16)

            load_expert(1)
            load_expert(2)
            sp.wait_ge(zeros_set, 1)
            sp.dma_start(scratch.rearrange("(p t c) d -> p t (c d)", p=P, c=ZROWS),
                         zrow[:].rearrange("p (o c) -> p o c", o=1).to_broadcast([P, SORTED // ZROWS, ZROWS * ROW])).then_inc(s_zero, 16)
            for e in range(3, EXPERTS):
                sp.wait_ge(w_lo[e - 3], 1)
                load_expert(e)
            def load_tile(t, q):
                place = sp.value_load(place_of[0:1, bass.ds(t, 1)], min_val=0, max_val=SORTED - 1)
                sp.dma_start(xs[:, q, :], scr_tiles[bass.ds(place, 1)].rearrange("o p c -> (o p) c")).then_inc(s_xs[q], 16)

            for b in range(BATCH - 1):
                store_base(sp, b, s_base)
            sp.wait_ge(places_ready, 1)
            sp.wait_ge(s_sort, 16 * NT)
            for t in range(2):
                load_tile(t, t)
            with sp.Fori(1, TILES // 2) as i:
                for q in range(2):
                    t = 2 * i + q
                    sp.wait_ge(xs_T, t - 1)
                    sp.wait_ge(dgate, t - 1)
                    sp.wait_ge(dtok, t - 1)
                    load_tile(t, q)

        @block.gpsimd
        def _(pool):
            pool.memset(ident[:], 0.0).then_inc(c_ones, 1)
            pool.memset(ones_bf[:], 1.0).then_inc(c_ones, 1)
            pool.memset(minus_half[:], -0.5).then_inc(c_ones, 1)
            pool.memset(one[:], 1.0).then_inc(c_ones, 1)
            pool.wait_ge(c_ones, 4)
            pool.affine_select(out=ident[:], in_=ident[:], compare_op=ALU.not_equal, fill=1.0, base=0,
                               pattern=[[-1, P]], channel_multiplier=1).then_inc(c_id, 1)
            pool.affine_select(out=tri[:], in_=ones_bf[:], compare_op=ALU.is_ge, fill=0.0, base=-1,
                               pattern=[[1, P]], channel_multiplier=-1).then_inc(c_pool, 1)
            pool.memset(half_pi[:], math.pi / 2).then_inc(c_pool, 1)
            pool.memset(zrow[:], 0.0).then_inc(zeros_set, 1)
            for b in range(BATCH):
                of = slice(b * TB, (b + 1) * TB)
                pool.wait_ge(ln1_var, b + 1)
                pool.tensor_tensor(rstd[:, of], vpe[:, of], minus_half[:, of], ALU.pow).then_inc(ln1_rstd, 1)
            pool.iota(eidx[:], pattern=[[0, TB], [1, NE]], base=0, channel_multiplier=0,
                      allow_small_or_imprecise_dtypes=True).then_inc(c_pool, 1)
            pool.iota(starts[:], pattern=[[REGION, NE]], base=0, channel_multiplier=0,
                      allow_small_or_imprecise_dtypes=True).then_inc(c_pool, 1)
            pool.iota(tno[:], pattern=[[1, TILES], [0, NE]], base=0, channel_multiplier=0,
                      allow_small_or_imprecise_dtypes=True).then_inc(c_pool, 1)
            pool.iota(pay[:, :, DIM + 1:DIM + 2], pattern=[[P, NT], [0, 1]], base=-TOKENS_OFF, channel_multiplier=1,
                      allow_small_or_imprecise_dtypes=True).then_inc(tok_set, 1)
            pool.wait_ge(c_pool, 5)
            pool.tensor_copy(seen[:], starts[:]).then_inc(seen_set, 1)
            pool.tensor_scalar(magic_starts[:], starts[:], MAGIC, None, ALU.add).then_inc(seen_set, 1)
            pool.wait_ge(s_v, 16)

            def base(b):
                pool.wait_ge(xn_ready, b + 1)
                xb, wide = tiles(xt, b), [P, TB, DIM]
                pool.tensor_tensor(xnD[:, b % 2, :, :], tiles(xn, b), row[:, 0:1, :].to_broadcast(wide), ALU.mult).then_inc(pstep, 1)
                pool.tensor_tensor(xb, xb, row[:, 1:2, :].to_broadcast(wide), ALU.add).then_inc(pstep, 1)
                pool.wait_ge(pstep, 2 * b + 2)
                pool.tensor_tensor(xb, xb, xnD[:, b % 2, :, :], ALU.add).then_inc(base_done, 1)

            def sort_rows(b):
                pool.wait_ge(pay_gate, b + 1)
                pool.wait_ge(pay_done, b + 1)
                pool.wait_ge(pos_ready, b + 1)
                for j in range(b * TB, (b + 1) * TB):
                    pool.indirect_dma_start(scratch, bass.IndirectOffsetOnAxis(pos_i[:, j:j + 1], 0),
                                            pay[:, j, :], None).then_inc(s_sort, 16)

            def content_sin(b):
                pool.wait_ge(cont_done, b + 1)
                pool.wait_ge(sin_done, b + 1)
                if b >= 2:
                    pool.wait_ge(mi_done, b - 1)
                    pool.wait_ge(ret_done, b - 1)
                pool.tensor_tensor(csn[b % 2][:], batch(cont, b), sn[b % 2][:], ALU.mult).then_inc(csn_done, 1)

            def content_cos(b):
                pool.wait_ge(cos_done, b + 1)
                pool.tensor_tensor(cc[b % 2][:], batch(cont, b), cs[b % 2][:], ALU.mult).then_inc(cc_done, 1)

            def retrieved_sin(b):
                pool.wait_ge(mi_done, b + 1)
                pool.tensor_tensor(mis[:], mi[:], sn[b % 2][:], ALU.mult).then_inc(mis_done, 1)

            def rstd2(b):
                pool.wait_ge(ln2_var, b + 1)
                pool.tensor_tensor(rstd[:, 0:TB], vpe[:, 0:TB], minus_half[:, 0:TB], ALU.pow).then_inc(ln2_rstd, 1)

            base(0)
            base(1)
            content_sin(0)
            content_cos(0)
            retrieved_sin(0)
            content_sin(1)
            content_cos(1)
            low_parts(pool, 2)
            rstd2(0)
            retrieved_sin(1)
            content_sin(2)
            content_cos(2)
            base(2)
            rstd2(1)
            content_sin(3)
            content_cos(3)
            retrieved_sin(2)
            pool.wait_ge(tok_set, 1)
            pool.wait_ge(s_zero, 16)
            sort_rows(0)
            rstd2(2)
            low_parts(pool, 3)
            retrieved_sin(3)
            base(3)
            low_parts(pool, 4)
            rstd2(3)
            sort_rows(1)
            low_parts(pool, 5)
            sort_rows(2)
            sort_rows(BATCH - 1)
            low_parts(pool, 6)
            store_base(pool, BATCH - 1, s_base_last)
            pool.wait_ge(s_base, 16 * (BATCH - 1))
            pool.wait_ge(s_base_last, 16)
            for t in range(TILES):
                pool.wait_ge(dtok, t + 1)
                pool.wait_ge(dy, t + 1)
                pool.indirect_dma_start(out, bass.IndirectOffsetOnAxis(ytok[:, t:t + 1], 0),
                                        ys[:, t * DIM:(t + 1) * DIM], None, bounds_check=TOKENS - 1,
                                        oob_is_err=False, compute_op=ALU.add).then_inc(s_out, 16)
            pool.wait_ge(s_out, 16 * TILES)

        @block.scalar
        def _(act):
            act.dma_start(wd[:], w_dt).then_inc(s_wd, 16)
            act.dma_start(wa[:], w_att).then_inc(s_w, 16)
            def load_table(which):
                act.add_instruction(mybir.InstLoadActFuncSet(
                    name=nc.get_next_instruction_name(), act_func_set_id=which, ins=[], outs=[]))

            load_table(SET_LN_EXP)
            act.wait_ge(wdt_mm, 1)
            act.activation(wdt[:], bank[6][:, 0:DIM], ACT.Copy).then_inc(wdt_sb, 1)

            def keep_turned(b):
                act.wait_ge(xn_T, b + 1)
                act.activation(batch(xnT, b), bank[4 * (b % 2)][:], ACT.Copy).then_inc(xnT_ready, 1)

            def softplus(b):
                act.wait_ge(dt_mm, b + 1)
                act.wait_ge(bdt_sb, 1)
                act.activation(r_abs[:], bank[DT_BANK[b]][:], ACT.Abs, bias=bdt[:, 0:1]).then_inc(abs_done, 1)
                act.wait_ge(abs_done, b + 1)
                act.activation(batch(r_log, b), r_abs[:], ACT.Exp, scale=-1.0).then_inc(exp_done, 1)
                act.wait_ge(exp_done, b + 1)
                act.activation(batch(r_log, b), batch(r_log, b), ACT.Ln, bias=1.0).then_inc(log_done, 1)

            keep_turned(0)
            keep_turned(1)
            softplus(0)
            keep_turned(2)
            softplus(1)
            keep_turned(3)
            softplus(2)
            softplus(3)
            load_table(SET_SILU_SIN)

            def phase(b):
                act.wait_ge(nf_done, b + 1)
                if b:
                    act.wait_ge(cos_done, b)
                if b >= 2:
                    act.wait_ge(ret_done, b - 1)
                act.activation(naf[:], nf[:], ACT.Abs).then_inc(naf_done, 1)
                act.activation(sn[b % 2][:], nf[:], ACT.Sin, scale=-TWO_PI).then_inc(sin_done, 1)
                act.wait_ge(naf_done, b + 1)
                act.activation(cs[b % 2][:], naf[:], ACT.Sin, scale=-TWO_PI, bias=half_pi[:, 0:1]).then_inc(cos_done, 1)

            def high_parts(e):
                q = (e - 1) % 2
                act.wait_ge(s_st[q], 16 * ((e + 1) // 2))
                act.activation(wx[:, e - 1, :, 0, :], stage[:, q, :].rearrange("p (c n) -> p c n", n=P), ACT.Copy).then_inc(w_hi, 1)

            def keep_norm(b):
                act.wait_ge(xn2_T, b + 1)
                if b:
                    act.wait_ge(lg_mm, b)
                act.activation(xn2S[:], bank[5][:], ACT.Copy).then_inc(xn2S_ready, 1)
                act.activation(batch(xn2T, b), bank[5][:], ACT.Copy).then_inc(xn2T_ready, 1)
                act.wait_ge(xn2_done, b + 1)
                act.activation(tiles(pay, b)[:, :, 0:DIM], xn2[:], ACT.Copy).then_inc(pay_done, 1)

            def silu0(b, k):
                act.wait_ge(h_mm, KF * b + k + 1)
                if b or k >= 2:
                    act.wait_ge(h_done, KF * b + k - 1)
                act.activation(sil[:, k % 2, :], bank[2 * (k % 2)][:], ACT.Silu).then_inc(sil_done, 1)

            def keep_y0(b):
                act.wait_ge(down0_mm, KF * (b + 1))
                if b:
                    act.wait_ge(y0_T, b)
                act.activation(y0T[:], bank[DOWN0_BANK[b]][:], ACT.Copy).then_inc(y0T_ready, 1)

            def exponentials(b):
                load_table(SET_LN_EXP)
                act.wait_ge(z_ready, b + 1)
                act.activation(tiles(ex, b), tiles(ex, b), ACT.Exp).then_inc(rt_exp, 1)
                load_table(SET_SILU_SIN)

            act.wait_ge(c_pool, 2)
            phase(0)
            phase(1)
            high_parts(1)
            high_parts(2)
            phase(2)
            keep_norm(0)
            exponentials(0)
            high_parts(3)
            for b in range(1, BATCH):
                if b + 2 < BATCH:
                    phase(b + 2)
                silu0(b - 1, 0)
                silu0(b - 1, 1)
                silu0(b - 1, 2)
                keep_norm(b)
                if b >= 2:
                    high_parts(b + 3)
                silu0(b - 1, 3)
                exponentials(b)
                keep_y0(b - 1)
                if b == 1:
                    high_parts(4)
            b = BATCH - 1
            silu0(b, 0)
            silu0(b, 1)
            high_parts(7)
            silu0(b, 2)
            silu0(b, 3)
            keep_y0(b)

            def turn_x(t, q, i, first=False):
                hold(act)
                act.wait_ge(xs_T, t + 1)
                act.wait_ge(s_xs[q], 16 * (i + 1))
                if not first:
                    act.wait_ge(dh_mm, t - 1)
                act.activation(xh[:, q, :], bank[5][:, 0:P], ACT.Copy).then_inc(xh_ready, 1)
                act.activation(gt[:, bass.ds(t, 1)], xs[:, q, DIM:DIM + 1], ACT.Copy).then_inc(dgate, 1)

            def high_h(t, q, first=False):
                act.wait_ge(dh_T, t + 1)
                if not first:
                    act.wait_ge(dy_mm, t - 1)
                act.activation(hh[:, q, :], bank[4 + 2 * q][:], ACT.Copy).then_inc(hh_ready, 1)

            def silu(t, q, first=False):
                act.wait_ge(dh1_mm, t + 1)
                if not first:
                    act.wait_ge(dh, t - 1)
                act.activation(sil[:, q, :], bank[2 * q][:], ACT.Silu).then_inc(dsil, 1)

            def keep_y(t, q):
                hold(act)
                act.wait_ge(dy_mm, t + 1)
                act.wait_ge(dgate, t + 1)
                act.activation(ys[:, bass.ds(t * DIM, DIM)], bank[7][:, 0:DIM], ACT.Copy,
                               scale=gt[:, bass.ds(t, 1)]).then_inc(dy_high, 1)

            turn_x(0, 0, 0, True)
            turn_x(1, 1, 0, True)
            silu(0, 0, True)
            turn_x(2, 0, 1)
            high_h(0, 0, True)
            silu(1, 1, True)
            turn_x(3, 1, 1)
            high_h(1, 1, True)
            silu(2, 0)
            keep_y(0, 0)
            with act.Fori(0, (TILES - 4) // UNROLL) as i:
                for n in range(UNROLL):
                    t, q = UNROLL * i + 3 + n, (3 + n) % 2
                    turn_x(t + 1, 1 - q, UNROLL // 2 * i + (4 + n) // 2)
                    high_h(t - 1, 1 - q)
                    silu(t, q)
                    keep_y(t - 2, q)
            t = TILES - 1
            high_h(t - 1, 0)
            silu(t, 1)
            keep_y(t - 2, 1)
            high_h(t, 1)
            keep_y(t - 1, 0)
            keep_y(t, 1)

        @block.tensor
        def _(pe):
            mm = pe.matmul
            pe.wait_ge(s_wd, 16)
            mm(bank[6][:, 0:DIM], wd1t, wd2, start=True, stop=True)
            mm(bank[6][:, DIM:DIM + 1], wd2, bd1, start=True, stop=True).then_inc(wdt_mm, 1)
            pe.wait_ge(c_id, 1)

            def turn(b):
                pe.wait_ge(xn_ready, b + 1)
                if b >= 2:
                    pe.wait_ge(xnT_ready, b - 1)
                for j in range(TB):
                    last = pe.transpose(bank[4 * (b % 2)][:, j * P:(j + 1) * P], xn[:, b * TB + j, :], ident[:])
                last.then_inc(xn_T, 1)

            def project_dt(b):
                pe.wait_ge(xnT_ready, b + 1)
                mm(bank[DT_BANK[b]][:], wdt[:], batch(xnT, b), start=True, stop=True).then_inc(dt_mm, 1)

            def project_b(b):
                pe.wait_ge(s_w, 16)
                if b >= 2:
                    pe.wait_ge(abs_done, b - 1)
                    pe.wait_ge(pos_done, b - 1)
                mm(bank[B_BANK[b]][:], wB, batch(xnT, b), start=True, stop=True).then_inc(b_mm, 1)

            def project_c(b):
                if b:
                    pe.wait_ge(x2_done, b)
                else:
                    pe.wait_ge(xnT_ready, 3)
                mm(bank[4][:], wC, batch(xnT, b), start=True, stop=True).then_inc(c_mm, 1)

            turn(0)
            turn(1)
            pe.wait_ge(wdt_sb, 1)
            pe.wait_ge(bdt_sb, 1)
            project_dt(0)
            turn(2)
            project_dt(1)
            project_b(0)
            turn(3)
            project_dt(2)
            project_b(1)
            project_dt(3)
            project_b(2)
            project_b(3)
            project_c(0)

            def out_proj(b):
                pe.wait_ge(ret_done, b + 1)
                for j in range(TB):
                    last = mm(bank[4][:, j * DIM:(j + 1) * DIM], ret[:, j * P:(j + 1) * P], wO, start=True, stop=True)
                last.then_inc(y_mm, 1)

            def turn2(b):
                pe.wait_ge(xn2_done, b + 1)
                if b:
                    pe.wait_ge(xn2T_ready, b)
                else:
                    pe.wait_ge(abs_done, BATCH)
                    pe.wait_ge(pos_done, BATCH)
                for j in range(TB):
                    last = pe.transpose(bank[5][:, j * P:(j + 1) * P], xn2[:, j, :], ident[:])
                last.then_inc(xn2_T, 1)

            def logits(b):
                pe.wait_ge(xn2S_ready, b + 1)
                if b:
                    pe.wait_ge(z_ready, b)
                    pe.wait_ge(rank_read, b)
                for j in range(TB):
                    last = mm(bank[6][:, j * EXPERTS:(j + 1) * EXPERTS], xn2S[:, j * P:(j + 1) * P], wR, start=True, stop=True)
                last.then_inc(lg_mm, 1)

            def hidden0(b, k):
                if k == 0:
                    pe.wait_ge(xn2T_ready, b + 1)
                if b or k >= 2:
                    pe.wait_ge(h_done, KF * b + k - 1)
                pair = 2 * (k % 2)
                mm(bank[pair][:], w_e0[:, k * P:(k + 1) * P], batch(xn2T, b), start=True, stop=True)
                mm(bank[pair + 1][:], w_e0[:, FF + k * P:FF + (k + 1) * P], batch(xn2T, b), start=True, stop=True).then_inc(h_mm, 1)

            def down0(b, k):
                pe.wait_ge(h_done, KF * b + k + 1)
                if k == 0:
                    if b == BATCH - 1:
                        pe.wait_ge(x2_done, BATCH)
                    elif b:
                        pe.wait_ge(base_out, b)
                mm(bank[DOWN0_BANK[b]][:], w_e0[:, 2 * FF + k * DIM:2 * FF + (k + 1) * DIM], hT0[:, k, :],
                   start=(k == 0), stop=(k == KF - 1)).then_inc(down0_mm, 1)

            def turn_y0(b):
                pe.wait_ge(y0T_ready, b + 1)
                for j in range(TB):
                    last = pe.transpose(bank[DOWN0_BANK[b]][:, j * P:(j + 1) * P], y0T[:, j * P:(j + 1) * P], ident[:])
                last.then_inc(y0_T, 1)

            def ranks(b):
                pe.wait_ge(oh_done, b + 1)
                pe.wait_ge(z_ready, b + 1)
                if b:
                    pe.wait_ge(seen_done, b)
                else:
                    pe.wait_ge(seen_set, 1)
                at = RANKS_AT
                past = seen[:].rearrange("p (o e) -> p o e", o=1).to_broadcast([P, TB, NE])
                mm(bank[6][:, at:at + TB * NE], tri[:], tiles(oh, b), start=True, stop=False)
                mm(bank[6][:, at:at + TB * NE], ones_bf[:], past, start=False, stop=False)
                for j in range(TB - 1):
                    after = oh[:, b * TB + j:b * TB + j + 1, :].to_broadcast([P, TB - 1 - j, NE])
                    last = mm(bank[6][:, at + (j + 1) * NE:at + TB * NE], ones_bf[:], after, start=False, stop=(j == TB - 2))
                if b == BATCH - 1:
                    at += TB * NE
                    mm(bank[6][:, at:at + NE], ones_bf[:], seen[:], start=True, stop=False)
                    for j in range(TB):
                        last = mm(bank[6][:, at:at + NE], ones_bf[:], oh[:, b * TB + j, :], start=False, stop=(j == TB - 1))
                last.then_inc(rank_mm, 1)

            out_proj(0)
            project_c(1)
            turn2(0)
            logits(0)
            out_proj(1)
            pe.wait_ge(s_e0, 16)
            pe.wait_ge(cont_done, BATCH)
            for b in range(1, BATCH):
                if b >= 2:
                    turn_y0(b - 2)
                hidden0(b - 1, 0)
                ranks(b - 1)
                hidden0(b - 1, 1)
                if b + 1 < BATCH:
                    project_c(b + 1)
                down0(b - 1, 0)
                hidden0(b - 1, 2)
                turn2(b)
                down0(b - 1, 1)
                logits(b)
                hidden0(b - 1, 3)
                if b + 1 < BATCH:
                    out_proj(b + 1)
                else:
                    ranks(b)
                down0(b - 1, 2)
                down0(b - 1, 3)
            b = BATCH - 1
            hidden0(b, 0)
            turn_y0(b - 1)
            hidden0(b, 1)
            for k in range(KF):
                down0(b, k)
                if k + 2 < KF:
                    hidden0(b, k + 2)

            def turn_x(t, q, i, first=False):
                pe.wait_ge(s_xs[q], 16 * (i + 1))
                pe.transpose(bank[5][:, 0:P], xs[:, q, 0:DIM], ident[:]).then_inc(xs_T, 1)

            PARTS = ((0, 0), (1, 0), (0, 1))

            def up(bk, m, e, t, q):
                for n, (low, part) in enumerate(PARTS):
                    w = wx[:, bass.ds(e, 1), m * KF:(m + 1) * KF, part, :].rearrange("p o c n -> p (o c) n")
                    last = mm(bank[bk][:], (xh, xl)[low][:, q, :], w, start=(n == 0), stop=(n == 2))
                return last

            def expert(t):
                return pe.value_load(expert_of[0:1, bass.ds(t, 1)], min_val=0, max_val=NE - 1)

            def turn_h(t, q, first=False):
                pe.wait_ge(dh, t + 1)
                for k in range(KF):
                    last = pe.transpose(bank[4 + 2 * q][:, k * P:(k + 1) * P], hN[:, q, k * P:(k + 1) * P], ident[:])
                last.then_inc(dh_T, 1)

            def down(t, q, e, first=False):
                pe.wait_ge(hl_ready, t + 1)
                if not first:
                    pe.wait_ge(dy, t)
                for k in range(KF):
                    w = wx[:, bass.ds(e, 1), 2 * KF + k, :, :].rearrange("p o c n -> p (o c n)")
                    high_w = wx[:, bass.ds(e, 1), 2 * KF + k, 0, :].rearrange("p o n -> p (o n)")
                    mm(bank[7][:, 0:2 * DIM], hh[:, q, k * P:(k + 1) * P], w, start=(k == 0), stop=False)
                    last = mm(bank[7][:, 0:DIM], hl[:, q, k * P:(k + 1) * P], high_w, start=False, stop=(k == KF - 1))
                last.then_inc(dy_mm, 1)

            def tile_step(t, q, i_next, e, number=2, more=True):
                pe.wait_ge(xl_ready, t + 1)
                up(2 * q, 0, e, t, q).then_inc(dh1_mm, 1)
                if more:
                    turn_x(t + 1, 1 - q, i_next)
                if number == 1:
                    pe.wait_ge(base_out, BATCH)
                if number:
                    turn_h(t - 1, 1 - q, number == 1)
                up(2 * q + 1, 1, e, t, q).then_inc(dh_mm, 1)

            pe.wait_ge(experts_ready, 1)
            for low in w_lo:
                pe.wait_ge(low, 1)
            turn_x(0, 0, 0, True)
            experts = [expert(0)]
            tile_step(0, 0, 0, experts[0], number=0)
            turn_y0(BATCH - 1)
            experts += [expert(1), expert(2)]
            tile_step(1, 1, 1, experts[1], number=1)
            tile_step(2, 0, 1, experts[2])
            down(0, 0, experts[0], True)
            with pe.Fori(0, (TILES - 4) // UNROLL) as i:
                experts = [expert(UNROLL * i + 3)]
                for n in range(UNROLL):
                    t = UNROLL * i + 3 + n
                    tile_step(t, (3 + n) % 2, UNROLL // 2 * i + (4 + n) // 2, experts[n])
                    if n + 1 < UNROLL:
                        experts.append(expert(t + 1))
                    down(t - 2, (3 + n) % 2, experts[n - 2] if n >= 2 else expert(t - 2))
            t = TILES - 1
            last = expert(t)
            tile_step(t, 1, 0, last, more=False)
            down(t - 2, 1, expert(t - 2))
            turn_h(t, 1)
            down(t - 1, 0, expert(t - 1))
            down(t, 1, last)

        @block.vector
        def _(dve):
            count = [0]

            def link(ins):
                count[0] += 1
                ins.then_inc(dstep, 1)
                dve.wait_ge(dstep, count[0])

            def mark(ins):
                count[0] += 1
                ins.then_inc(dstep, 1)
                return count[0]

            def statistics(of):
                for j in range(of.start, of.stop):
                    last = dve.bn_aggr(mv[:, j, :], st[:, j, :])
                link(last)
                return dve.tensor_scalar(vpe[:, of], mv[:, of, 1:2].rearrange("p n o -> p (n o)"), EPS, None, ALU.add)

            def statistics1(b):
                dve.wait_ge(s_xb[b], 16)
                of = slice(b * TB, (b + 1) * TB)
                for j in range(b * TB, (b + 1) * TB):
                    last = dve.bn_stats(st[:, j:j + 1, :], xt[:, j:j + 1, :])
                link(last)
                statistics(of).then_inc(ln1_var, 1)

            def normalise(b):
                dve.wait_ge(ln1_rstd, b + 1)
                for j in range(b * TB, (b + 1) * TB):
                    last = dve.tensor_scalar(xn[:, j, :], xt[:, j, :], mv[:, j, 0:1], rstd[:, j:j + 1],
                                             ALU.subtract, ALU.mult)
                last.then_inc(xn_ready, 1)

            def positive(b):
                dve.wait_ge(abs_done, b + 1)
                dve.tensor_scalar(batch(r_pos, b), bank[DT_BANK[b]][:], bdt[:, 0:1], 0.0, ALU.add, ALU.max).then_inc(pos_done, 1)

            def contents(b):
                dve.wait_ge(b_mm, b + 1)
                dve.scalar_tensor_tensor(out=batch(cont, b), in0=bank[B_BANK[b]][:], scalar=vec[:, 0:1], in1=batch(xnT, b),
                                         op0=ALU.add, op1=ALU.mult).then_inc(cont_done, 1)

            statistics1(0)
            statistics1(1)
            normalise(0)
            statistics1(2)
            normalise(1)
            dve.wait_ge(wdt_sb, 1)
            dve.wait_ge(s_w, 16)
            dve.tensor_tensor(bdt[:], bank[6][:, DIM:DIM + 1], vec[:, 2:3], ALU.add).then_inc(bdt_sb, 1)
            dve.tensor_scalar(turn[:], vec[:, 3:4], 1.0 / (2.0 * math.pi), None, ALU.mult).then_inc(c_dve, 1)
            statistics1(3)
            normalise(2)
            normalise(3)

            def phases_and_residual(p, r):
                if p is not None:
                    dve.wait_ge(log_done, p + 1)
                    dve.wait_ge(pos_done, p + 1)
                    summed = mark(dve.tensor_tensor_scan(cum[:], batch(r_pos, p), batch(r_log, p), 0.0, ALU.add, ALU.add))
                if r is not None:
                    dve.wait_ge(y_mm, r + 1)
                    dve.wait_ge(base_done, r + 1)
                    dve.tensor_tensor(tiles(x2, r), bank[4][:].rearrange("p (j d) -> p j d", j=TB), tiles(xt, r),
                                      ALU.add).then_inc(x2_done, 1)
                if p is not None:
                    dve.wait_ge(dstep, summed)
                    dve.tensor_scalar(tph[:], cum[:], turn[:, 0:1], None, ALU.mult)
                    rounded = mark(dve.tensor_scalar(kph[:], cum[:], turn[:, 0:1], MAGIC, ALU.mult, ALU.add))
                if r is not None:
                    dve.wait_ge(x2_done, r + 1)
                    for j in range(TB):
                        last = dve.bn_stats(st[:, j:j + 1, :], x2[:, r * TB + j:r * TB + j + 1, :])
                    taken = mark(last)
                if p is not None:
                    dve.wait_ge(dstep, rounded)
                    if p:
                        dve.wait_ge(sin_done, p)
                        dve.wait_ge(naf_done, p)
                    dve.scalar_tensor_tensor(out=nf[:], in0=kph[:], scalar=MAGIC, in1=tph[:],
                                             op0=ALU.subtract, op1=ALU.subtract).then_inc(nf_done, 1)
                if r is not None:
                    dve.wait_ge(dstep, taken)
                    statistics(slice(0, TB)).then_inc(ln2_var, 1)

            def memory_sin(b):
                dve.wait_ge(csn_done, b + 1)
                if b:
                    dve.wait_ge(mis_done, b)
                dve.tensor_tensor_scan(mi[:], one[:], csn[b % 2][:], 0.0, ALU.mult, ALU.add).then_inc(mi_done, 1)

            def memory_cos(b):
                dve.wait_ge(cc_done, b + 1)
                link(dve.tensor_tensor_scan(mr[:], one[:], cc[b % 2][:], 0.0, ALU.mult, ALU.add))

            def normalise2(b):
                dve.wait_ge(ln2_rstd, b + 1)
                if b:
                    dve.wait_ge(xn2_T, b)
                    dve.wait_ge(pay_done, b)
                for j in range(TB):
                    last = dve.tensor_scalar(xn2[:, j, :], x2[:, b * TB + j, :], mv[:, j, 0:1], rstd[:, j:j + 1],
                                             ALU.subtract, ALU.mult)
                last.then_inc(xn2_done, 1)

            def over(t, n):
                return t[:].rearrange("p (j o) -> p j o", o=1).to_broadcast([P, TB, n])

            def retrieve_and_choose(r, c):
                if r is not None:
                    cos_part = mark(dve.tensor_tensor(cc[r % 2][:], mr[:], cs[r % 2][:], ALU.mult))
                if c is not None:
                    dve.wait_ge(lg_mm, c + 1)
                    lg, exc = bank[6][:, 0:TB * EXPERTS].rearrange("p (j e) -> p j e", j=TB), tiles(ex, c)
                    chosen = lg[:, :, 1:EXPERTS]
                    largest = mark(dve.tensor_reduce(mx7[:], chosen, AX.X, ALU.max))
                if r is not None:
                    dve.wait_ge(dstep, cos_part)
                    dve.wait_ge(mis_done, r + 1)
                    both = mark(dve.tensor_tensor(mr[:], cc[r % 2][:], mis[:], ALU.add))
                if c is not None:
                    dve.wait_ge(dstep, largest)
                    dve.tensor_tensor(mx8[:], lg[:, :, 0:1].rearrange("p j o -> p (j o)"), mx7[:], ALU.max)
                    equal = mark(dve.tensor_tensor(eq[:], chosen, over(mx7, NE), ALU.is_equal))
                if r is not None:
                    dve.wait_ge(dstep, both)
                    dve.wait_ge(c_mm, r + 1)
                    if r:
                        dve.wait_ge(y_mm, r)
                    dve.scalar_tensor_tensor(out=ret[:], in0=bank[4][:], scalar=vec[:, 1:2], in1=mr[:],
                                             op0=ALU.add, op1=ALU.mult).then_inc(ret_done, 1)
                if c is not None:
                    dve.wait_ge(dstep, equal)
                    dve.tensor_tensor(exc[:, :, EXPERTS:EXPERTS + 1].rearrange("p j o -> p (j o)"), mx7[:], mx8[:], ALU.subtract)
                    firsts = mark(dve.scalar_tensor_tensor(out=eq[:], in0=eq[:], scalar=-16.0, in1=eidx[:], op0=ALU.mult, op1=ALU.add))
                    dve.tensor_tensor(exc[:, :, 0:EXPERTS], lg, over(mx8, EXPERTS), ALU.subtract).then_inc(z_ready, 1)
                    dve.wait_ge(dstep, firsts)
                    link(dve.tensor_reduce(mn[:], eq[:], AX.X, ALU.min))
                    dve.tensor_tensor(tiles(oh, c), eq[:], over(mn, NE), ALU.is_equal).then_inc(oh_done, 1)

            def positions(b):
                dve.wait_ge(rank_mm, b + 1)
                rank = bank[6][:, RANKS_AT:RANKS_AT + TB * NE].rearrange("p (j e) -> p j e", j=TB)
                dve.tensor_tensor(pos3[:], rank, tiles(oh, b), ALU.mult).then_inc(rank_read, 1)
                more = mark(dve.tensor_reduce(seen_b[:], tiles(oh, b).rearrange("p j e -> p e j"), AX.X, ALU.add))
                dve.wait_ge(rank_read, b + 1)
                at = mark(dve.tensor_reduce(pos[:], pos3[:], AX.X, ALU.add))
                dve.wait_ge(dstep, more)
                dve.tensor_tensor(seen[:], seen[:], seen_b[:], ALU.add).then_inc(seen_done, 1)
                dve.wait_ge(dstep, at)
                dve.tensor_copy(pos_i[:, b * TB:(b + 1) * TB], pos[:]).then_inc(pos_ready, 1)

            def add_expert0(b, j):
                if j == 0:
                    dve.wait_ge(y0_T, b + 1)
                at = b * TB + j
                last = dve.scalar_tensor_tensor(out=y0[:, at, :], in0=bank[DOWN0_BANK[b]][:, j * P:(j + 1) * P],
                                                scalar=g0[:, at:at + 1], in1=x2[:, at, :], op0=ALU.mult, op1=ALU.add)
                if j == TB - 1:
                    last.then_inc(base_out, 1)

            def gates(b, beside=None):
                def other(j):
                    if beside is not None:
                        add_expert0(beside, j)

                exb = tiles(ex, b)
                two = [pr[:, :, n:n + 1].rearrange("p j o -> p (j o)") for n in range(2)]
                dve.wait_ge(rt_exp, b + 1)
                n = mark(dve.tensor_reduce(zs[:], exb[:, :, 0:EXPERTS], AX.X, ALU.add))
                other(0)
                dve.wait_ge(dstep, n)
                n = mark(dve.reciprocal(zs[:], zs[:]))
                other(1)
                dve.wait_ge(dstep, n)
                dve.tensor_tensor(pr[:, :, 0:1], exb[:, :, 0:1], over(zs, 1), ALU.mult)
                n = mark(dve.tensor_tensor(pr[:, :, 1:2], exb[:, :, EXPERTS:EXPERTS + 1], over(zs, 1), ALU.mult))
                other(2)
                dve.wait_ge(dstep, n)
                n = mark(dve.tensor_tensor(gs[:], two[0], two[1], ALU.add))
                other(3)
                dve.wait_ge(dstep, n)
                link(dve.tensor_scalar(gs[:], gs[:], 1e-9, None, ALU.max))
                link(dve.reciprocal(gs[:], gs[:]))
                dve.tensor_tensor(tiles(pay, b)[:, :, DIM:DIM + 1].rearrange("p j o -> p (j o)"), two[1], gs[:],
                                  ALU.mult).then_inc(pay_gate, 1)
                link(dve.tensor_tensor(g0[:, b * TB:(b + 1) * TB], two[0], gs[:], ALU.mult))

            def hidden0(b, k):
                dve.wait_ge(sil_done, KF * b + k + 1)
                if b:
                    dve.wait_ge(down0_mm, KF * (b - 1) + k + 1)
                dve.tensor_tensor(hT0[:, k, :], sil[:, k % 2, :], bank[2 * (k % 2) + 1][:], ALU.mult).then_inc(h_done, 1)

            dve.wait_ge(c_dve, 1)
            dve.wait_ge(c_ones, 4)
            positive(0)
            phases_and_residual(0, None)
            positive(1)
            contents(0)
            positive(2)
            contents(1)
            positive(3)
            contents(2)
            contents(3)
            phases_and_residual(1, None)
            memory_sin(0)
            memory_cos(0)
            retrieve_and_choose(0, None)
            dve.wait_ge(c_pool, 5)
            dve.wait_ge(seen_set, 2)
            low_parts(dve, 1)
            phases_and_residual(2, 0)
            normalise2(0)
            memory_sin(1)
            memory_cos(1)
            retrieve_and_choose(1, 0)
            for b in range(1, BATCH):
                after = b + 1 if b + 1 < BATCH else None
                phases_and_residual(b + 2 if b + 2 < BATCH else None, b)
                gates(b - 1, b - 2 if b >= 2 else None)
                hidden0(b - 1, 0)
                normalise2(b)
                positions(b - 1)
                if after:
                    memory_sin(after)
                hidden0(b - 1, 1)
                if after:
                    memory_cos(after)
                hidden0(b - 1, 2)
                retrieve_and_choose(after, b)
                if b == BATCH - 1:
                    positions(b)
                hidden0(b - 1, 3)
            b = BATCH - 1
            gates(b)
            hidden0(b, 0)
            at = RANKS_AT + TB * NE
            link(dve.tensor_scalar(ntile[:], bank[6][:, at:at + NE], 1.0 / P, (P - 1.0) / P - 0.5 + 0.5 / P, ALU.mult, ALU.add))
            link(dve.tensor_scalar(ntile[:], ntile[:], MAGIC, None, ALU.add))
            link(dve.tensor_tensor(ntile[:], ntile[:], magic_starts[:], ALU.subtract))
            for j in range(TB):
                add_expert0(b - 1, j)
            hidden0(b, 1)
            link(dve.tensor_tensor_scan(tends[:], one[:, 0:NE], ntile[:], 0.0, ALU.mult, ALU.add))
            ends, skips = (t[:].rearrange("p (o e) -> p o e", o=1).to_broadcast([P, TILES, NE]) for t in (tends, spare_tiles))
            dve.tensor_scalar(spare_tiles[:], ntile[:], -1.0, float(REGION), ALU.mult, ALU.add)
            link(dve.tensor_tensor(tcmp[:], tno[:], ends, ALU.is_ge))
            link(dve.tensor_reduce(texp[:], tcmp[:], AX.X, ALU.add))
            dve.tensor_scalar(expert_of[:], texp[:], NE - 1.0, None, ALU.min).then_inc(experts_ready, 1)
            link(dve.tensor_tensor(tcmp[:], tcmp[:], skips, ALU.mult))
            link(dve.tensor_reduce(tskip[:], tcmp[:], AX.X, ALU.add))
            dve.tensor_tensor(place_of[:], tskip[:], tno[:, :, 0:1].rearrange("p t o -> p (t o)"), ALU.add).then_inc(places_ready, 1)
            hidden0(b, 2)
            low_parts(dve, NE)
            hidden0(b, 3)

            def token(t, q, i):
                dve.wait_ge(s_xs[q], 16 * (i + 1))
                dve.tensor_scalar(ytok[:, bass.ds(t, 1)], xs[:, q, DIM + 1:DIM + 2], float(TOKENS_OFF), None,
                                  ALU.add).then_inc(dtok, 1)

            def low_x(t, q, first=False):
                dve.wait_ge(xh_ready, t + 1)
                if not first:
                    dve.wait_ge(dh_mm, t - 1)
                dve.tensor_tensor(xl[:, q, :], bank[5][:, 0:P], xh[:, q, :].bitcast(F32), ALU.subtract).then_inc(xl_ready, 1)

            def low_h(t, q, first=False):
                dve.wait_ge(hh_ready, t + 1)
                if not first:
                    dve.wait_ge(dy_mm, t - 1)
                dve.tensor_tensor(hl[:, q, :], bank[4 + 2 * q][:], hh[:, q, :].bitcast(F32), ALU.subtract).then_inc(hl_ready, 1)

            def hidden(t, q, first=False):
                dve.wait_ge(dsil, t + 1)
                dve.wait_ge(dh_mm, t + 1)
                if not first:
                    dve.wait_ge(dh_T, t - 1)
                dve.tensor_tensor(hN[:, q, :], sil[:, q, :], bank[2 * q + 1][:], ALU.mult).then_inc(dh, 1)

            def finish_y(t):
                dve.wait_ge(dy_high, t + 1)
                at = bass.ds(t * DIM, DIM)
                dve.scalar_tensor_tensor(out=ys[:, at], in0=bank[7][:, DIM:2 * DIM], scalar=gt[:, bass.ds(t, 1)],
                                         in1=ys[:, at], op0=ALU.mult, op1=ALU.add).then_inc(dy, 1)

            token(0, 0, 0)
            low_x(0, 0, True)
            token(1, 1, 0)
            low_x(1, 1, True)
            for j in range(TB):
                add_expert0(BATCH - 1, j)
            hidden(0, 0, True)
            token(2, 0, 1)
            low_x(2, 0)
            low_h(0, 0, True)
            hidden(1, 1, True)
            token(3, 1, 1)
            low_x(3, 1)
            low_h(1, 1, True)
            hidden(2, 0)
            with dve.Fori(0, (TILES - 4) // UNROLL) as i:
                for n in range(UNROLL):
                    t, q = UNROLL * i + 3 + n, (3 + n) % 2
                    finish_y(t - 3)
                    token(t + 1, 1 - q, UNROLL // 2 * i + (4 + n) // 2)
                    low_x(t + 1, 1 - q)
                    low_h(t - 1, 1 - q)
                    hidden(t, q)
            t = TILES - 1
            finish_y(t - 3)
            low_h(t - 1, 0)
            hidden(t, 1)
            finish_y(t - 2)
            low_h(t, 1)
            finish_y(t - 1)
            finish_y(t)


_OUT = (BATCH, SEQ, DIM)


def kernel(**a):
    import concourse.bacc as _bacc
    from concourse.bass_utils import run_bass_kernel_spmd as _run

    def col(v):
        return np.ascontiguousarray(np.asarray(v).reshape(-1, 1))

    w1, w2, w3 = (np.asarray(a["L0_ffn_" + n]) for n in ("W1", "W2", "W3"))
    put = {
        "x": np.asarray(a["L0_attn_x"]).reshape(TOKENS, DIM),
        "rows": np.stack([np.asarray(a["L0_attn_D"]), np.asarray(a["L0_attn_b_out"])]),
        "w_dt": np.concatenate([np.asarray(a["L0_attn_W_dt1"]).T, np.asarray(a["L0_attn_W_dt2"]),
                                col(a["L0_attn_b_dt1"])], axis=1),
        "w_att": np.concatenate([np.asarray(a["L0_attn_" + n]) for n in ("W_B", "W_C", "W_out")]
                                + [np.asarray(a["L0_ffn_Wr"]).T]
                                + [col(a["L0_attn_" + n]) for n in ("b_B", "b_C", "b_dt2", "omega_base")], axis=1),
        "w_ff": np.stack([w1.transpose(2, 0, 1), w3.transpose(2, 0, 1),
                          w2.reshape(EXPERTS, DIM, KF, P).transpose(3, 0, 2, 1).reshape(P, EXPERTS, FF)],
                         axis=2).reshape(P, EXPERTS * 3 * FF),
    }
    nc = _bacc.Bacc("TRN2", target_bir_lowering=False, num_devices=1)
    arrays, args = {}, []
    for name, v in put.items():
        v = np.ascontiguousarray(v)
        arrays[name + "_in"] = v
        args.append(nc.dram_tensor(name + "_in", v.shape, mybir.dt.from_np(v.dtype), kind="ExternalInput").ap())
    out = nc.dram_tensor("out_0", [TOKENS, DIM], F32, kind="ExternalOutput").ap()
    scratch = nc.dram_tensor("sorted_rows", [SORTED * P, ROW], F32, kind="Internal").ap()
    build(nc, *args, out, scratch)
    r = _run(nc, [arrays], core_ids=[0])
    return r.results[0]["out_0"].reshape(_OUT)
```
